# Optimizing a Trainium2 kernel written in Bass

```python
import numpy as np
import jax
import jax.numpy as jnp

def _softmax(x, axis=-1):
    return jax.nn.softmax(x, axis=axis)

def _gelu(x):
    return jax.nn.gelu(x, approximate=True)

def _silu(x):
    return jax.nn.silu(x)

def _sigmoid(x):
    return jax.nn.sigmoid(x)

def _layernorm(x, axis=-1, eps=1e-05):
    m = jnp.mean(x, axis=axis, keepdims=True)
    v = jnp.var(x, axis=axis, keepdims=True)
    return (x - m) / jnp.sqrt(v + eps)

def _scatter_add(tgt, idx, src, axis=0):
    return tgt.at[idx].add(src)

def _segment_sum(src, seg, n):
    return jax.ops.segment_sum(src, seg, n)
kernel_name = 'mk_gnn_resnorm_d4_gnn_r32_606249'

def setup_inputs(seed: int=0):
    np.random.seed(seed)
    _w = jnp.asarray

    def _rec_inputs():
        import jax
        import jax.numpy as jnp
        _gk = jax.random.key(seed)
        x = -0.000202 + 1 * jax.random.normal(jax.random.fold_in(_gk, 1), (50000, 128), jnp.float32)
        src = jax.random.randint(jax.random.fold_in(_gk, 2), (50000,), 0, 50000, jnp.int32)
        dst = jax.random.randint(jax.random.fold_in(_gk, 3), (50000,), 0, 50000, jnp.int32)
        _o = jnp.argsort(dst, stable=True)
        src = src[_o]
        dst = dst[_o]
        edge_weight = jax.random.uniform(jax.random.fold_in(_gk, 13), (50000,), jnp.float32, 0.0, 0.999998)
        return (x, src, dst, edge_weight)
    x, src, dst, edge_weight = _rec_inputs()

    def _L0_gnn_setup():
        import jax, jax.numpy as jnp
        import numpy as np
        N_NODES = 50000
        N_EDGES = 50000
        D = 128
        NEG_SLOPE = 0.01
        key = jax.random.key(seed)
        ks = jax.random.split(key, 8)
        features = jax.random.normal(ks[0], (N_NODES, D), dtype=jnp.float32)
        edge_index = jax.random.randint(ks[1], (2, N_EDGES), 0, N_NODES, dtype=jnp.int64)
        W = jax.random.normal(ks[2], (D, D), dtype=jnp.float32) * (1.0 / np.sqrt(D))
        b = jax.random.normal(ks[3], (D,), dtype=jnp.float32) * 0.01
        a1_w = jax.random.normal(ks[4], (D,), dtype=jnp.float32) * (1.0 / np.sqrt(D))
        a1_b = jax.random.normal(ks[5], (1,), dtype=jnp.float32) * 0.01
        a2_w = jax.random.normal(ks[6], (D,), dtype=jnp.float32) * (1.0 / np.sqrt(D))
        a2_b = jax.random.normal(ks[7], (1,), dtype=jnp.float32) * 0.01
        return {'features': features, 'edge_index': edge_index, 'W': W, 'b': b, 'a1_w': a1_w, 'a1_b': a1_b, 'a2_w': a2_w, 'a2_b': a2_b}
    _L0_gnn_all = _L0_gnn_setup()
    _L0_gnn_in = {k: v for k, v in _L0_gnn_all.items() if k in ('W', 'b', 'a1_w', 'a1_b', 'a2_w', 'a2_b')}
    del _L0_gnn_all

    def _L1_gnn_setup():
        import jax, jax.numpy as jnp
        import numpy as np
        EPS = 1e-07
        N_NODES, N_EDGES, D = (10000, 5000, 128)

        def mobius_add(x, y):
            x2 = jnp.sum(x * x, axis=-1, keepdims=True)
            y2 = jnp.sum(y * y, axis=-1, keepdims=True)
            xy = jnp.sum(x * y, axis=-1, keepdims=True)
            num = (1.0 + 2.0 * xy + y2) * x + (1.0 - x2) * y
            den = 1.0 + 2.0 * xy + x2 * y2
            return num / jnp.maximum(den, EPS)

        def mobius_scalar_mul(r, x):
            nrm = jnp.sqrt(jnp.sum(x * x, axis=-1, keepdims=True))
            nrm_c = jnp.clip(nrm, EPS, 1.0 - EPS)
            scaled = jnp.tanh(r * jnp.arctanh(nrm_c)) * (x / nrm_c)
            return jnp.where(nrm > EPS, scaled, jnp.zeros_like(x))
        key = jax.random.key(seed)
        kx, ke = jax.random.split(key)
        raw = jax.random.normal(kx, (N_NODES, D), dtype=jnp.float32)
        x = 0.4 * raw / (1.0 + jnp.linalg.norm(raw, axis=-1, keepdims=True))
        edge_index = jax.random.randint(ke, (2, N_EDGES), 0, N_NODES, dtype=jnp.int64)
        return {'x': x, 'edge_index': edge_index}
    _L1_gnn_all = _L1_gnn_setup()
    _L1_gnn_in = {k: v for k, v in _L1_gnn_all.items() if k in ()}
    del _L1_gnn_all

    def _L2_gnn_setup():
        import jax, jax.numpy as jnp
        import numpy as np
        N = 3125
        E = 50000
        D = 128
        key = jax.random.key(seed)
        ks = jax.random.split(key, 8)
        x = jax.random.normal(ks[0], (N, D), dtype=jnp.float32)
        edge_index = jax.random.randint(ks[1], (2, E), 0, N, dtype=jnp.int32)
        scale = 1.0 / np.sqrt(2 * D)
        W0 = jax.random.normal(ks[2], (2 * D, D), dtype=jnp.float32) * scale
        b0 = jax.random.normal(ks[3], (D,), dtype=jnp.float32) * scale
        W1 = jax.random.normal(ks[4], (2 * D, D), dtype=jnp.float32) * scale
        b1 = jax.random.normal(ks[5], (D,), dtype=jnp.float32) * scale
        W2 = jax.random.normal(ks[6], (2 * D, D), dtype=jnp.float32) * scale
        b2 = jax.random.normal(ks[7], (D,), dtype=jnp.float32) * scale
        return {'x': x, 'edge_index': edge_index, 'W0': W0, 'b0': b0, 'W1': W1, 'b1': b1, 'W2': W2, 'b2': b2}
    _L2_gnn_all = _L2_gnn_setup()
    _L2_gnn_in = {k: v for k, v in _L2_gnn_all.items() if k in ('W0', 'b0', 'W1', 'b1', 'W2', 'b2')}
    del _L2_gnn_all

    def _L3_gnn_setup():
        import jax, jax.numpy as jnp
        import numpy as np
        SDIM = 128
        DEPTH = 5
        CUTOFF = 5.0
        NUM_RADIAL = 32
        N_NODES = 50000
        N_EDGES = 12500

        def ssp(v):
            return jax.nn.softplus(v) - jnp.log(2.0).astype(v.dtype)
        key = jax.random.key(seed)
        ks = jax.random.split(key, 16)
        x = jax.random.normal(ks[0], (N_NODES, SDIM), dtype=jnp.float32)
        edge_index = jax.random.randint(ks[1], (2, N_EDGES), 0, N_NODES, dtype=jnp.int64)
        edge_attr = jax.random.uniform(ks[2], (N_EDGES,), dtype=jnp.float32)
        batch = jnp.sort(jax.random.randint(ks[3], (N_NODES,), 0, 64, dtype=jnp.int64))
        s = 1.0 / np.sqrt(SDIM)
        sr = 1.0 / np.sqrt(NUM_RADIAL)
        return {'x': x, 'edge_attr': edge_attr, 'fw1': jax.random.normal(ks[4], (DEPTH, NUM_RADIAL, SDIM), dtype=jnp.float32) * sr, 'fb1': jnp.zeros((DEPTH, SDIM), dtype=jnp.float32), 'fw2': jax.random.normal(ks[5], (DEPTH, SDIM, SDIM), dtype=jnp.float32) * s, 'fb2': jnp.zeros((DEPTH, SDIM), dtype=jnp.float32), 'lin1_w': jax.random.normal(ks[6], (DEPTH, SDIM, SDIM), dtype=jnp.float32) * s, 'lin2_w': jax.random.normal(ks[7], (DEPTH, SDIM, SDIM), dtype=jnp.float32) * s, 'lin2_b': jnp.zeros((DEPTH, SDIM), dtype=jnp.float32), 'ln_g': jnp.ones((DEPTH, SDIM), dtype=jnp.float32), 'ln_b': jnp.zeros((DEPTH, SDIM), dtype=jnp.float32), 'edge_index': edge_index, 'batch': batch}
    _L3_gnn_all = _L3_gnn_setup()
    _L3_gnn_in = {k: v for k, v in _L3_gnn_all.items() if k in ('fw1', 'fb1', 'fw2', 'fb2', 'lin1_w', 'lin2_w', 'lin2_b', 'ln_g', 'ln_b')}
    del _L3_gnn_all
    return {'x': x, 'src': src, 'dst': dst, 'edge_weight': edge_weight, 'L0_gnn_W': _L0_gnn_in['W'], 'L0_gnn_b': _L0_gnn_in['b'], 'L0_gnn_a1_w': _L0_gnn_in['a1_w'], 'L0_gnn_a1_b': _L0_gnn_in['a1_b'], 'L0_gnn_a2_w': _L0_gnn_in['a2_w'], 'L0_gnn_a2_b': _L0_gnn_in['a2_b'], 'L2_gnn_W0': _L2_gnn_in['W0'], 'L2_gnn_b0': _L2_gnn_in['b0'], 'L2_gnn_W1': _L2_gnn_in['W1'], 'L2_gnn_b1': _L2_gnn_in['b1'], 'L2_gnn_W2': _L2_gnn_in['W2'], 'L2_gnn_b2': _L2_gnn_in['b2'], 'L3_gnn_fw1': _L3_gnn_in['fw1'], 'L3_gnn_fb1': _L3_gnn_in['fb1'], 'L3_gnn_fw2': _L3_gnn_in['fw2'], 'L3_gnn_fb2': _L3_gnn_in['fb2'], 'L3_gnn_lin1_w': _L3_gnn_in['lin1_w'], 'L3_gnn_lin2_w': _L3_gnn_in['lin2_w'], 'L3_gnn_lin2_b': _L3_gnn_in['lin2_b'], 'L3_gnn_ln_g': _L3_gnn_in['ln_g'], 'L3_gnn_ln_b': _L3_gnn_in['ln_b']}

def reference(x, src, dst, edge_weight, L0_gnn_W, L0_gnn_b, L0_gnn_a1_w, L0_gnn_a1_b, L0_gnn_a2_w, L0_gnn_a2_b, L2_gnn_W0, L2_gnn_b0, L2_gnn_W1, L2_gnn_b1, L2_gnn_W2, L2_gnn_b2, L3_gnn_fw1, L3_gnn_fb1, L3_gnn_fw2, L3_gnn_fb2, L3_gnn_lin1_w, L3_gnn_lin2_w, L3_gnn_lin2_b, L3_gnn_ln_g, L3_gnn_ln_b):
    import jax
    import jax.numpy as jnp

    def _L0_gnn_ref(features, edge_index, W, b, a1_w, a1_b, a2_w, a2_b):
        import jax, jax.numpy as jnp
        import numpy as np
        N_NODES = 50000
        N_EDGES = 50000
        D = 128
        NEG_SLOPE = 0.01
        n = features.shape[0]
        h = features @ W.T + b
        s1 = h @ a1_w + a1_b[0]
        s2 = h @ a2_w + a2_b[0]
        src = edge_index[0]
        dst = edge_index[1]
        e = s1[src] + s2[dst]
        e = jnp.where(e >= 0, e, NEG_SLOPE * e)
        m = jax.ops.segment_max(e, src, num_segments=n)
        ex = jnp.exp(e - m[src])
        denom = jax.ops.segment_sum(ex, src, num_segments=n)
        att = ex / denom[src]
        out = jax.ops.segment_sum(att[:, None] * h[dst], src, num_segments=n)
        return out

    def _L1_gnn_ref(x, edge_index):
        import jax, jax.numpy as jnp
        import numpy as np
        EPS = 1e-07
        N_NODES, N_EDGES, D = (10000, 5000, 128)

        def mobius_add(x, y):
            x2 = jnp.sum(x * x, axis=-1, keepdims=True)
            y2 = jnp.sum(y * y, axis=-1, keepdims=True)
            xy = jnp.sum(x * y, axis=-1, keepdims=True)
            num = (1.0 + 2.0 * xy + y2) * x + (1.0 - x2) * y
            den = 1.0 + 2.0 * xy + x2 * y2
            return num / jnp.maximum(den, EPS)

        def mobius_scalar_mul(r, x):
            nrm = jnp.sqrt(jnp.sum(x * x, axis=-1, keepdims=True))
            nrm_c = jnp.clip(nrm, EPS, 1.0 - EPS)
            scaled = jnp.tanh(r * jnp.arctanh(nrm_c)) * (x / nrm_c)
            return jnp.where(nrm > EPS, scaled, jnp.zeros_like(x))
        src, dst = (edge_index[0], edge_index[1])
        n, d = x.shape
        messages = mobius_add(x[src], -x[dst])

        def body(out, em):
            m, idx = em
            return (out.at[idx].set(mobius_add(out[idx], m)), None)
        out0 = jnp.zeros((n, d), dtype=x.dtype)
        total, _ = jax.lax.scan(body, out0, (messages, dst))
        count = jnp.zeros((n,), dtype=x.dtype).at[dst].add(1.0)
        scale = 1.0 / jnp.maximum(count, 1.0)
        aggr = mobius_scalar_mul(scale[:, None], total)
        return mobius_add(x, aggr)

    def _L2_gnn_ref(x, edge_index, W0, b0, W1, b1, W2, b2):
        import jax, jax.numpy as jnp
        import numpy as np
        N = 3125
        E = 50000
        D = 128
        src, dst = (edge_index[0], edge_index[1])
        n = x.shape[0]
        count = jax.ops.segment_sum(jnp.ones((src.shape[0],), dtype=x.dtype), dst, num_segments=n)
        inv = 1.0 / (count + 1.0)
        for W, b in ((W0, b0), (W1, b1), (W2, b2)):
            agg = jax.ops.segment_sum(x[src], dst, num_segments=n)
            neigh = agg * inv[:, None]
            x = jax.nn.relu(jnp.concatenate([x, neigh], axis=-1) @ W + b)
        return x

    def _L3_gnn_ref(x, edge_attr, fw1, fb1, fw2, fb2, lin1_w, lin2_w, lin2_b, ln_g, ln_b, edge_index, batch):
        import jax, jax.numpy as jnp
        import numpy as np
        SDIM = 128
        DEPTH = 5
        CUTOFF = 5.0
        NUM_RADIAL = 32
        N_NODES = 50000
        N_EDGES = 12500

        def ssp(v):
            return jax.nn.softplus(v) - jnp.log(2.0).astype(v.dtype)
        src, dst = (edge_index[0], edge_index[1])
        n = x.shape[0]
        offsets = jnp.linspace(0.0, CUTOFF, NUM_RADIAL, dtype=x.dtype)
        coeff = -0.5 / (offsets[1] - offsets[0]) ** 2
        rbf = jnp.exp(coeff * (edge_attr[:, None] - offsets[None, :]) ** 2)
        C = 0.5 * (jnp.cos(jnp.pi * edge_attr / CUTOFF) + 1.0) * (edge_attr < CUTOFF)
        deg = jax.ops.segment_sum(jnp.ones_like(edge_attr), dst, num_segments=n)
        denom = jnp.maximum(deg, 1.0)[:, None]
        for i in range(DEPTH):
            W = ssp(rbf @ fw1[i] + fb1[i]) @ fw2[i] + fb2[i]
            W = W * C[:, None]
            h = x @ lin1_w[i]
            msg = h[src] * W
            agg = jax.ops.segment_sum(msg, dst, num_segments=n) / denom
            x = x + ssp(agg) @ lin2_w[i] + lin2_b[i]
            mu = jnp.mean(x, axis=-1, keepdims=True)
            var = jnp.mean((x - mu) ** 2, axis=-1, keepdims=True)
            x = (x - mu) * jax.lax.rsqrt(var + 1e-05) * ln_g[i] + ln_b[i]
        return x
    edge_index = jnp.stack([src, dst])
    batch0 = jnp.zeros((50000,), jnp.int32)
    x = _layernorm(x + _L0_gnn_ref(x, edge_index, L0_gnn_W, L0_gnn_b, L0_gnn_a1_w, L0_gnn_a1_b, L0_gnn_a2_w, L0_gnn_a2_b), axis=-1)
    x = _layernorm(x + _L1_gnn_ref(x, edge_index), axis=-1)
    x = _layernorm(x + _L2_gnn_ref(x, edge_index, L2_gnn_W0, L2_gnn_b0, L2_gnn_W1, L2_gnn_b1, L2_gnn_W2, L2_gnn_b2), axis=-1)
    x = _layernorm(x + _L3_gnn_ref(x, edge_weight, L3_gnn_fw1, L3_gnn_fb1, L3_gnn_fw2, L3_gnn_fb2, L3_gnn_lin1_w, L3_gnn_lin2_w, L3_gnn_lin2_b, L3_gnn_ln_g, L3_gnn_ln_b, edge_index, batch0), axis=-1)
    return x

_drawn_inputs = setup_inputs


def setup_inputs(seed=0):
    import zlib

    import numpy as np

    out = dict(_drawn_inputs(seed))
    spreads = {'L3_gnn_fb1': (0.0, 0.414),
     'L3_gnn_fb2': (0.0, 0.1),
     'L3_gnn_lin2_b': (0.0, 0.1),
     'L3_gnn_ln_g': (1.0, 0.2),
     'L3_gnn_ln_b': (0.0, 0.1)}
    factors = {'L0_gnn_b': 8.0, 'L2_gnn_b0': 4.295}
    for name, (base, spread) in spreads.items():
        noise = np.random.default_rng([zlib.crc32(name.encode()), seed]).standard_normal(out[name].shape)
        drawn = base * np.exp(spread * noise) if base else spread * noise
        out[name] = jnp.asarray(drawn.astype(out[name].dtype))
    for name, factor in factors.items():
        out[name] = (out[name] * factor).astype(out[name].dtype)
    return out
```

```python
import numpy as np
import concourse.bass as bass
from concourse import mybir

ALU = mybir.AluOpType
ACT = mybir.ActivationFunctionType
F32 = mybir.dt.float32
BF16 = mybir.dt.bfloat16
I32 = mybir.dt.int32
U32 = mybir.dt.uint32
U16 = mybir.dt.uint16
AX_X = mybir.AxisListType.X

P = 128
D = 128
N = 50000
E = 50000
CUTOFF = 5.0
RADIAL = 32
NT = 392
J = 4
G = P * J
NG = NT // J
NR = NG * G
FULL = E // P
TAIL = E - FULL * P
CAP = 40
SHIFT = 18
COLS = 1 << SHIFT
FILL = 512
SPARE = 8
MAX_ITEMS = COLS // J - FILL // J - SPARE
IN_WORDS, OUT_WORDS = 2, 2
SKIP = 1 << 27


def stand(eng, sem_, value, held):
    eng.wait_ge(sem_, value)
    eng.sem_inc(held, 1)


class Chain:

    def __init__(self, eng, sem, base=0):
        self.eng, self.sem, self.base, self.n = eng, sem, base, 0

    def __call__(self, ins):
        ins.then_inc(self.sem, 1)
        self.n += 1
        return self.base + self.n

    def wait(self):
        self.eng.wait_ge(self.sem, self.base + self.n)

    def all(self, n):
        assert self.n == n, f"{self.n} instructions signal, not {n}"


def sem(nc, name):
    return nc.alloc_semaphore(f"{name}_{nc.next_id()}")


def sbuf(nc, name, shape, dt):
    return nc.alloc_sbuf_tensor(f"{name}_{nc.next_id()}", shape, dt)


def psum(nc, name, shape, dt):
    return nc.alloc_psum_tensor(f"{name}_{nc.next_id()}", shape, dt)


def constants(nc, k):
    k.ident = sbuf(nc, "ident", [P, P], F32)
    k.later = sbuf(nc, "later", [P, P], F32)
    k.ones = sbuf(nc, "ones", [P, NT], F32)
    k.zeros = sbuf(nc, "zeros", [P, FILL * IN_WORDS], F32)
    k.count_i = sbuf(nc, "count_i", [P, NT], I32)
    k.count = sbuf(nc, "count", [P, NT], F32)
    k.part_i = sbuf(nc, "part_i", [P, 1], I32)
    k.part = sbuf(nc, "part", [P, 1], F32)
    k.radial_i = sbuf(nc, "radial_i", [P, 1], I32)
    k.radial_of = sbuf(nc, "radial_of", [P, 1], F32)
    k.eps = sbuf(nc, "eps", [P, 1], F32)
    s_radial = sem(nc, "s_radial")
    s_iota = sem(nc, "s_iota")
    s_set = sem(nc, "s_set")
    with nc.Block() as block:
        @block.gpsimd
        def _(pool):
            pool.iota(k.count_i[:, :], [[1, NT]], base=0, channel_multiplier=0).then_inc(s_iota, 1)
            pool.iota(k.part_i[:, :], [[0, 1]], base=0, channel_multiplier=1).then_inc(s_iota, 1)
            pool.wait_ge(s_set, 3)
            pool.affine_select(out=k.ident[:, :], in_=k.ident[:, :], compare_op=ALU.not_equal, fill=1.0, base=0,
                               pattern=[[-1, P]], channel_multiplier=1)
            pool.affine_select(out=k.later[:, :], in_=k.later[:, :], compare_op=ALU.is_ge, fill=1.0, base=0,
                               pattern=[[-1, P]], channel_multiplier=1)

        @block.vector
        def _(dve):
            dve.memset(k.ident[:, :], 0.0).then_inc(s_set, 1)
            dve.memset(k.later[:, :], 0.0).then_inc(s_set, 1)
            dve.memset(k.ones[:, :], 1.0).then_inc(s_set, 1)
            dve.memset(k.zeros[:, :], 0.0)
            dve.memset(k.eps[:, :], 1e-5)
            dve.wait_ge(s_iota, 2)
            dve.tensor_copy(k.count[:, :], k.count_i[:, :])
            dve.tensor_copy(k.part[:, :], k.part_i[:, :])
            dve.tensor_scalar(k.radial_i[:, :], k.part_i[:, :], RADIAL - 1, None, ALU.bitwise_and
                              ).then_inc(s_radial, 1)
            dve.wait_ge(s_radial, 1)
            dve.tensor_copy(k.radial_of[:, :], k.radial_i[:, :])


def load_keys(nc, k):
    raw = [sbuf(nc, f"raw{q}", [P, 4, P], I32) for q in range(2)]
    part_i = [sbuf(nc, f"split_i{q}", [P, 2, 4 * P], I32) for q in range(2)]
    part_f = [sbuf(nc, f"split_f{q}", [P, 2, 4 * P], F32) for q in range(2)]
    turned = [psum(nc, f"turned{q}", [P, 2, 4 * P], F32) for q in range(2)]
    weight = sbuf(nc, "weight_rows", [P, 4, P], F32)
    turned_w = psum(nc, "turned_w", [P, 4 * P], F32)
    s_set = sem(nc, "s_set")
    s_raw = sem(nc, "s_raw")
    s_int = sem(nc, "s_int")
    s_split = sem(nc, "s_split")
    s_turned = sem(nc, "s_turned")
    s_low = sem(nc, "s_low")
    s_pad = sem(nc, "s_pad")
    with nc.Block() as block:
        @block.scalar
        def _(act):
            act.dma_start(k.x_pad[0:FULL * P, :].rearrange("(a b) d -> a (b d)", a=P), 
                          k.x[0:FULL * P, :].rearrange("(a b) d -> a (b d)", a=P)).then_inc(s_pad, 16)
            act.dma_start(k.x_pad[FULL * P:N, :], k.x[FULL * P:N, :]).then_inc(s_pad, 16)
            act.dma_start(k.x_pad[N:NR, :].rearrange("(p b) d -> p (b d)", b=2),
                          k.zeros[0:(NR - N) // 2, 0:2 * D]).then_inc(s_pad, 16)
            act.wait_ge(s_pad, 48)

        @block.sync
        def _(sp):
            sp.wait_ge(s_set, 3)
            for dst, src in ((raw[0], k.dst), (raw[1], k.src), (weight, k.edge_weight)):
                whole = src[0:3 * P * P].rearrange("(c q e) -> q c e", q=P, e=P)
                sp.dma_start(dst[:, 0:3, :], whole).then_inc(s_raw, 16)
                sp.dma_start(dst[0:FULL - 3 * P, 3, :],
                             src[3 * P * P:FULL * P].rearrange("(q e) -> q e", e=P)).then_inc(s_raw, 16)
                sp.dma_start(dst[FULL - 3 * P:FULL - 3 * P + 1, 3, 0:TAIL],
                             src[FULL * P:E].rearrange("(q e) -> q e", q=1)).then_inc(s_raw, 16)
            sp.wait_ge(s_split, 2)
            for q in range(2):
                sp.dma_start(k.low_rows[q].rearrange("(c q) e -> q c e", q=P),
                             part_f[q][:, 1, :].rearrange("q (c e) -> q c e", e=P)).then_inc(s_low, 16)
            sp.wait_ge(s_low, 32)

        @block.vector
        def _(dve):
            for q in range(2):
                dve.memset(raw[q][:, :, :], -P).then_inc(s_set, 1)
            dve.memset(weight[:, :, :], 0.0).then_inc(s_set, 1)
            dve.wait_ge(s_raw, 9 * 16)
            for q in range(2):
                flat = raw[q][:, :, :].rearrange("p c e -> p (c e)")
                dve.tensor_scalar(part_i[q][:, 0, :], flat, 7, None, ALU.arith_shift_right).then_inc(s_int, 1)
                dve.tensor_scalar(part_i[q][:, 1, :], flat, P - 1, None, ALU.bitwise_and).then_inc(s_int, 1)
            dve.wait_ge(s_int, 4)
            for q in range(2):
                dve.tensor_copy(part_f[q][:, :, :], part_i[q][:, :, :]).then_inc(s_split, 1)
            dve.wait_ge(s_turned, 2)
            for q in range(2):
                dve.tensor_copy(k.high[q][:, :], turned[q][:, 0, 0:NT])
                dve.tensor_copy(k.low[q][:, :], turned[q][:, 1, 0:NT])
            dve.wait_ge(s_turned, 3)
            dve.tensor_copy(k.weight[:, :], turned_w[:, 0:NT])

        @block.tensor
        def _(pe):
            for q in range(2):
                pe.wait_ge(s_split, q + 1)
                for h in range(2):
                    for c in range(4):
                        last = pe.transpose(turned[q][:, h, c * P:(c + 1) * P], part_f[q][:, h, c * P:(c + 1) * P],
                                            k.ident[:, :])
                last.then_inc(s_turned, 1)
            for c in range(4):
                last = pe.transpose(turned_w[:, c * P:(c + 1) * P], weight[:, c, :], k.ident[:, :])
            last.then_inc(s_turned, 1)


def rank_edges(nc, k):
    U = 2
    KQ = [(u, q) for u in range(U) for q in range(2)]
    buf = lambda name, shape, dt: {a: sbuf(nc, f"{name}{a[0]}{a[1]}", shape, dt) for a in KQ}
    low_row = buf("low_row", [P, P], F32)
    is_high = buf("is_high", [P, NT], BF16)
    is_low = buf("is_low", [P, P], BF16)
    low_is = buf("low_is", [P, P], F32)
    earlier = buf("earlier", [P, P], BF16)
    snap = buf("snap", [P, NT], F32)
    waste = buf("waste", [P, NT], F32)
    table = [psum(nc, f"table{q}", [P, 512], F32) for q in range(2)]
    found = {a: psum(nc, f"found{a[0]}{a[1]}", [P, 512], F32) for a in KQ}
    s_row = {a: sem(nc, f"s_row{a[0]}{a[1]}") for a in KQ}
    s_hot, s_snap, s_found, s_grown, s_ranked = [
        [sem(nc, f"{n}{q}") for q in range(2)] for n in ("s_hot", "s_snap", "s_found", "s_grown", "s_ranked")]
    s_zero = sem(nc, "s_zero")
    with nc.Block() as block:
        @block.sync
        def _(sp):
            with sp.Fori(0, NT // U) as i:
                for u, q in KQ:
                    stand(sp, s_hot[q], i * U + u + 1, k.held)
                    sp.dma_start(low_row[u, q][:, :],
                                 k.low_rows[q][bass.ds(i * U + u, 1), :].rearrange("a e -> (a e)").partition_broadcast(P)
                                 ).then_inc(s_row[u, q], 16)

        @block.vector
        def _(dve):
            dve.memset(waste[0, 0][:, :], 0.0).then_inc(s_zero, 1)
            for q in range(2):
                dve.memset(waste[1, q][0:1, 0:1], 0.0).then_inc(s_hot[q], U)
                dve.memset(waste[1, q][0:1, 1:2], 0.0).then_inc(s_ranked[q], U)

            def one_hots(i, u):
                t = i * U + u
                for q in range(2):
                    high = k.high[q][:, bass.ds(t, 1)]
                    low = k.low[q][:, bass.ds(t, 1)]
                    dve.wait_ge(s_grown[q], t + 1)
                    dve.wait_ge(s_ranked[q], t + 1)
                    dve.tensor_scalar(is_high[u, q][:, :], k.count[:, :], high, None, ALU.is_equal)
                    dve.tensor_scalar(is_low[u, q][:, :], k.count[:, 0:P], low, None, ALU.is_equal)
                    dve.wait_ge(s_row[u, q], i * 16 + 16)
                    dve.tensor_scalar(low_is[u, q][:, :], low_row[u, q][:, :], k.part[:, 0:1], None, ALU.is_equal)
                    dve.scalar_tensor_tensor(out=earlier[u, q][:, :], in0=low_row[u, q][:, :], scalar=low,
                                             in1=k.later[:, :], op0=ALU.is_equal, op1=ALU.mult).then_inc(s_hot[q], 1)

            def ranks(i, u):
                t = i * U + u
                for q in range(2):
                    dve.wait_ge(s_found[q], t + 1)
                    dve.scalar_tensor_tensor(out=waste[u, q][:, :], in0=found[u, q][:, 0:NT], scalar=1.0,
                                             in1=is_high[u, q][:, :], op0=ALU.mult, op1=ALU.mult,
                                             accum_out=k.rank[q][:, bass.ds(t, 1)]).then_inc(s_ranked[q], 1)

            one_hots(0, 0)
            with dve.Fori(0, NT // U - 1) as i:
                one_hots(i, 1)
                ranks(i, 0)
                one_hots(i + 1, 0)
                ranks(i, 1)
            one_hots(NT // U - 1, 1)
            for u in range(U):
                ranks(NT // U - 1, u)
            for q in range(2):
                dve.wait_ge(s_grown[q], NT + U)
                dve.tensor_copy(k.degree[q][:, :], table[q][:, 0:NT])

        @block.scalar
        def _(act):
            act.preload_act_table_set("natural_log_exp_and_others")
            with act.Fori(0, NT // U) as i:
                for u, q in KQ:
                    act.wait_ge(s_grown[q], i * U + u + U)
                    act.activation(snap[u, q][:, :], table[q][:, 0:NT], ACT.Copy).then_inc(s_snap[q], 1)

        @block.tensor
        def _(pe):
            pe.wait_ge(s_zero, 1)
            for q in range(2):
                pe.matmul(table[q][:, 0:NT], k.ident[:, :], waste[0, 0][:, :], start=True, stop=True,
                          ).then_inc(s_grown[q], U)
            with pe.Fori(0, NT // U) as i:
                for u, q in KQ:
                    t = i * U + u
                    pe.wait_ge(s_snap[q], t + 1)
                    pe.wait_ge(s_hot[q], t + 1 + U)
                    pe.wait_ge(s_ranked[q], t + 1)
                    pe.matmul(found[u, q][:, 0:NT], low_is[u, q][:, :], snap[u, q][:, :], start=True, stop=False)
                    pe.matmul(found[u, q][:, 0:NT], earlier[u, q][:, :], is_high[u, q][:, :], start=False, stop=True
                              ).then_inc(s_found[q], 1)
                    pe.matmul(table[q][:, 0:NT], is_low[u, q][:, :], is_high[u, q][:, :], start=False, stop=True,
                              skip_group_check=True).then_inc(s_grown[q], 1)


def sort_nodes(nc, k):
    B = CAP + 1
    W = NT + P
    two = lambda name, shape, dt: [sbuf(nc, f"{name}{q}", shape, dt) for q in range(2)]
    capped = two("capped", [P, NT], F32)
    member = two("member", [P, NT], F32)
    prefix = two("prefix", [P, NT], F32)
    part_pos = two("part_pos", [P, NT], F32)
    position = two("position", [P, NT], F32)
    row_count = two("row_count", [P, B], F32)
    total_sb = two("total_sb", [P, B], F32)
    upto = two("upto", [P, B], F32)
    offset = two("offset", [P, B], F32)
    reach = two("reach", [P, B + 1], F32)
    reach_i = two("reach_i", [P, B + 1], I32)
    most = two("most", [P, 1], F32)
    most_row = two("most_row", [1, 1], F32)
    extra = two("extra", [P, 1], F32)
    group = two("group", [P, W], F32)
    first = two("first", [P, W], F32)
    more = two("more", [P, W], F32)
    pos_i = two("pos_i", [P, NT], I32)
    group_i = two("group_i", [P, NT], I32)
    slot_i = two("slot_i", [P, NT], I32)
    slot_f = two("slot_f", [P, NT], F32)
    key_f = two("key_f", [P, NT], F32)
    past = sbuf(nc, "past", [P, NT], F32)
    small = [psum(nc, f"small{q}", [P, 512], F32) for q in range(2)]
    turn = [psum(nc, f"turn{q}", [P, 512], F32) for q in range(2)]
    spread = [psum(nc, f"spread{q}", [P, 512], F32) for q in range(2)]
    s_dve = sem(nc, "s_dve")
    s_count = sem(nc, "s_count")
    s_place = sem(nc, "s_place")
    s_first = sem(nc, "s_first")
    s_rows = sem(nc, "s_rows")
    s_sum = sem(nc, "s_sum")
    s_most = sem(nc, "s_most")
    s_turn = sem(nc, "s_turn")
    s_spread = sem(nc, "s_spread")
    with nc.Block() as block:
        @block.tensor
        def _(pe):
            for q in range(2):
                pe.wait_ge(s_rows, q + 1)
                pe.matmul(small[q][:, 0:B], k.later[:, :], row_count[q][:, :], start=True, stop=True)
                pe.matmul(small[q][:, 64:64 + B], k.ones[:, 0:P], row_count[q][:, :], start=True, stop=True
                          ).then_inc(s_sum, 1)
            for q in range(2):
                pe.wait_ge(s_most, q + 1)
                pe.transpose(turn[q][0:1, 0:P], most[q][:, 0:1], k.ident[:, :]).then_inc(s_turn, 1)
            for q in range(2):
                pe.wait_ge(s_most, 2 + q + 1)
                pe.matmul(spread[q][:, 0:1], k.ones[0:1, 0:P], most_row[q][0:1, 0:1], start=True, stop=True
                          ).then_inc(s_spread, 1)

        @block.vector
        def _(dve):
            c = Chain(dve, s_dve)
            for q in range(2):
                c(dve.tensor_scalar(capped[q][:, :], k.degree[q][:, :], float(CAP), None, ALU.min))
                c(dve.memset(position[q][:, :], 0.0))
            c.wait()
            with dve.Fori(0, B) as b:
                for q in range(2):
                    dve.wait_ge(s_count, b * 2 + q)
                    dve.scalar_tensor_tensor(out=member[0][:, :], in0=capped[q][:, :], scalar=k.count[:, bass.ds(b, 1)],
                                             in1=k.ones[:, :], op0=ALU.is_equal, op1=ALU.mult,
                                             accum_out=row_count[q][:, bass.ds(b, 1)]).then_inc(s_count, 1)
            dve.wait_ge(s_count, 2 * B)
            for q in range(2):
                dve.sem_inc(s_rows, 1)
            for q in range(2):
                c(dve.tensor_reduce(most[q][:, :], k.degree[q][:, :], AX_X, ALU.max))
            c.wait()
            for q in range(2):
                dve.sem_inc(s_most, 1)
            dve.wait_ge(s_turn, 2)
            for q in range(2):
                dve.tensor_reduce(most_row[q][:, :], turn[q][0:1, 0:P], AX_X, ALU.max).then_inc(s_most, 1)
            dve.wait_ge(s_sum, 2)
            for q in range(2):
                c(dve.tensor_copy(total_sb[q][:, :], small[q][:, 64:64 + B]))
            c.wait()
            for q in range(2):
                c(dve.tensor_tensor_scan(upto[q][:, :], k.ones[:, 0:B], total_sb[q][:, :], 0.0, ALU.mult, ALU.add))
            c.wait()
            for q in range(2):
                c(dve.tensor_scalar(reach[q][:, 0:B], upto[q][:, :], -1.0, float(NR), ALU.mult, ALU.add))
                c(dve.tensor_copy(reach[q][:, B:B + 1], total_sb[q][:, CAP:B]))
            c.wait()
            for q in range(2):
                c(dve.scalar_tensor_tensor(out=offset[q][:, :], in0=small[q][:, 0:B], scalar=-1.0,
                                           in1=reach[q][:, 0:B], op0=ALU.add, op1=ALU.add))
            c.wait()
            for q in range(2):
                c(dve.tensor_scalar(reach[q][:, :], reach[q][:, :], float(G - 1), None, ALU.add))
            c.wait()
            with dve.Fori(0, B) as b:
                for q in range(2):
                    dve.wait_ge(s_place, b * 8 + q)
                    dve.tensor_scalar(member[q][:, :], capped[q][:, :], k.count[:, bass.ds(b, 1)], None, ALU.is_equal
                                      ).then_inc(s_place, 1)
                for q in range(2):
                    dve.wait_ge(s_place, b * 8 + 1 + q)
                    dve.tensor_tensor_scan(prefix[q][:, :], k.ones[:, :], member[q][:, :], 0.0, ALU.mult, ALU.add
                                           ).then_inc(s_place, 1)
                for q in range(2):
                    dve.wait_ge(s_place, b * 8 + 3 + q)
                    dve.scalar_tensor_tensor(out=part_pos[q][:, :], in0=prefix[q][:, :],
                                             scalar=offset[q][:, bass.ds(b, 1)], in1=member[q][:, :],
                                             op0=ALU.add, op1=ALU.mult).then_inc(s_place, 1)
                for q in range(2):
                    dve.wait_ge(s_place, b * 8 + 5 + q)
                    dve.tensor_tensor(position[q][:, :], position[q][:, :], part_pos[q][:, :], ALU.add
                                      ).then_inc(s_place, 1)
            dve.wait_ge(s_place, 8 * B)
            dve.wait_ge(s_spread, 2)
            for q in range(2):
                c(dve.tensor_copy(reach_i[q][:, :], reach[q][:, :]))
                c(dve.tensor_copy(pos_i[q][:, :], position[q][:, :]))
                c(dve.tensor_scalar(extra[q][:, :], spread[q][:, 0:1], -float(CAP), 0.0, ALU.add, ALU.max))
                c(dve.tensor_copy(group[q][:, NT:W], k.count[:, 0:P]))
            c.wait()
            for q in range(2):
                c(dve.tensor_scalar(reach_i[q][:, :], reach_i[q][:, :], 9, None, ALU.arith_shift_right))
                c(dve.tensor_scalar(group_i[q][:, :], pos_i[q][:, :], 9, None, ALU.arith_shift_right))
                c(dve.tensor_scalar(slot_i[q][:, :], pos_i[q][:, :], J - 1, None, ALU.bitwise_and))
                c(dve.tensor_scalar(k.lane[q][:, :], pos_i[q][:, :], (P - 1) * J, SHIFT - 2, ALU.bitwise_and,
                                    ALU.logical_shift_left))
            c.wait()
            for q in range(2):
                c(dve.tensor_copy(reach[q][:, :], reach_i[q][:, :]))
                c(dve.tensor_copy(group[q][:, 0:NT], group_i[q][:, :]))
                c(dve.tensor_copy(slot_f[q][:, :], slot_i[q][:, :]))
            c.wait()
            for q in range(2):
                c(dve.memset(first[q][:, :], 0.0))
                c(dve.tensor_scalar(more[q][:, :], group[q][:, :], reach[q][:, B:B + 1], extra[q][:, 0:1],
                                    ALU.min, ALU.mult))
            c.wait()
            dve.memset(key_f[0][:, 0:1], 0.0).then_inc(s_first, 1)
            with dve.Fori(0, CAP) as r:
                for q in range(2):
                    dve.wait_ge(s_first, r * 2 + q + 1)
                    dve.scalar_tensor_tensor(out=first[q][:, :], in0=group[q][:, :], scalar=reach[q][:, bass.ds(r, 1)],
                                             in1=first[q][:, :], op0=ALU.min, op1=ALU.add).then_inc(s_first, 1)
            dve.wait_ge(s_first, 2 * CAP + 1)
            for q in range(2):
                c(dve.tensor_tensor(first[q][:, :], first[q][:, :], more[q][:, :], ALU.add))
            c.wait()
            for q in range(2):
                c(dve.tensor_copy(k.start[q][:, :], first[q][0:1, NT:W]))
                c(dve.scalar_tensor_tensor(out=k.column[q][:, :], in0=first[q][:, 0:NT], scalar=float(J),
                                           in1=slot_f[q][:, :], op0=ALU.mult, op1=ALU.add))
                c(dve.scalar_tensor_tensor(out=key_f[q][:, :], in0=k.high[q][:, :], scalar=float(P),
                                           in1=k.low[q][:, :], op0=ALU.mult, op1=ALU.add))
            c(dve.tensor_scalar(k.row_d[:, :], position[0][:, :], 1.0, None, ALU.add))
            c(dve.tensor_scalar(k.row_s[:, :], position[1][:, :], 1.0, None, ALU.add))
            c(dve.memset(k.key[0][:, NT:NT + J], 0))
            c(dve.memset(k.key[1][:, NT:NT + J], 0))
            c(dve.tensor_scalar(past[:, :], k.high[0][:, :], 0.0, float(SKIP), ALU.is_lt, ALU.mult))
            c.wait()
            for q in range(2):
                c(dve.tensor_scalar(k.key[q][:, 0:NT], key_f[q][:, :], 0.0, None, ALU.max))
            c(dve.tensor_copy(k.past[:, :], past[:, :]))
            c.wait()


def project(nc, k):
    U = 2
    K = D + 2
    w_raw = sbuf(nc, "w_raw", [P, P], F32)
    w_ext = sbuf(nc, "w_ext", [P, K], F32)
    a_cols = sbuf(nc, "a_cols", [P, 2], F32)
    b_col = sbuf(nc, "b_col", [P, 1], F32)
    b_wide = sbuf(nc, "b_wide", [P, P], F32)
    a_bias = sbuf(nc, "a_bias", [P, 2], F32)
    bias = sbuf(nc, "bias", [P, K], F32)
    x = [sbuf(nc, f"x{u}", [P, J, k.XW], F32) for u in range(U)]
    xt = [sbuf(nc, f"xt{u}", [P, J * P], F32) for u in range(U)]
    h = [sbuf(nc, f"h{u}", [P, J, K], F32) for u in range(U)]
    to = [sbuf(nc, f"to{u}", [P, J], U32) for u in range(U)]
    turned = [psum(nc, f"turned{u}", [P, J * P], F32) for u in range(U)]
    prod = [psum(nc, f"prod{u}", [P, J, 256], F32) for u in range(U)]
    setup = psum(nc, "setup", [P, 512], F32)
    s_w = sem(nc, "s_w")
    s_wide = sem(nc, "s_wide")
    s_setup = sem(nc, "s_setup")
    s_ext = sem(nc, "s_ext")
    s_x = [sem(nc, f"s_x{u}") for u in range(U)]
    s_turned = sem(nc, "s_turned")
    s_xt = sem(nc, "s_xt")
    s_prod = sem(nc, "s_prod")
    s_h = sem(nc, "s_h")
    s_tag = sem(nc, "s_tag")
    s_out = [sem(nc, f"s_out{u}") for u in range(U)]
    s_sent = [sem(nc, f"s_sent{u}") for u in range(U)]
    s_zero = sem(nc, "s_zero")
    s_clear = sem(nc, "s_clear")
    with nc.Block() as block:
        @block.sync
        def _(sp):
            sp.dma_start(w_raw[:, :], k.L0_gnn_W).then_inc(s_w, 16)
            sp.dma_start(a_cols[:, 0:1], k.L0_gnn_a1_w.rearrange("(d a) -> d a", a=1)).then_inc(s_w, 16)
            sp.dma_start(a_cols[:, 1:2], k.L0_gnn_a2_w.rearrange("(d a) -> d a", a=1)).then_inc(s_w, 16)
            sp.dma_start(b_col[:, :], k.L0_gnn_b.rearrange("(d a) -> d a", a=1)).then_inc(s_w, 16)
            sp.dma_start(bias[:, 0:D], k.L0_gnn_b.partition_broadcast(P)).then_inc(s_w, 16)
            sp.dma_start(a_bias[:, 0:1], k.L0_gnn_a1_b.partition_broadcast(P)).then_inc(s_w, 16)
            sp.dma_start(a_bias[:, 1:2], k.L0_gnn_a2_b.partition_broadcast(P)).then_inc(s_w, 16)
            for table in (k.h0, k.mix, k.ya, k.yb, k.yc, k.ha, k.hb):
                sp.dma_start(table[0:1, 0:D], k.zeros[0:1, 0:D]).then_inc(s_zero, 16)
            sp.dma_start(k.xd[0:1, :], k.zeros[0:1, 0:k.XW]).then_inc(s_zero, 16)

            def load(i, u):
                    sp.dma_start(x[u][:, :, 0:D], k.x_pad[bass.ds((i * U + u) * G, G), :].rearrange("(j p) d -> p j d", p=P)
                                 ).then_inc(s_x[u], 16)

            for u in range(U):
                load(0, u)
            with sp.Fori(1, NG // U) as i:
                for u in range(U):
                    stand(sp, s_sent[u], i * 16 * J, k.held)
                    stand(sp, s_turned, i * U + u + 1, k.held)
                    load(i, u)
            sp.wait_ge(s_zero, 128)

        @block.gpsimd
        def _(pool):
            with pool.Fori(0, NG // U) as i:
                for u in range(U):
                    stand(pool, s_x[u], i * 16 + 16, k.held)
                    stand(pool, s_tag, i * U + u + 1, k.held)
                    for j in range(J):
                        pool.indirect_dma_start(k.xd[:, :], bass.IndirectOffsetOnAxis(ap=to[u][:, j:j + 1], axis=0),
                                                x[u][:, j, :], None, bounds_check=NR, oob_is_err=False
                                                ).then_inc(s_sent[u], 16)
            for u in range(U):
                pool.wait_ge(s_sent[u], 16 * J * (NG // U))

        @block.scalar
        def _(act):
            act.preload_act_table_set("natural_log_exp_and_others")
            with act.Fori(0, NG // U) as i:
                for u in range(U):
                    act.wait_ge(s_turned, i * U + u + 1 + U)
                    act.wait_ge(s_prod, i * U + u + 1)
                    act.activation(xt[u][:, :], turned[u][:, :], ACT.Copy).then_inc(s_xt, 1)
                    act.wait_ge(s_h, i * U + u + 1 + U)
                    act.dma_start(k.h0[bass.ds((i * U + u) * G + 1, G), :].rearrange("(j p) d -> p j d", p=P),
                                  h[u][:, :, 0:D]).then_inc(s_out[u], 16)
            for u in range(U):
                act.wait_ge(s_out[u], 16 * (NG // U))

        @block.tensor
        def _(pe):
            pe.wait_ge(s_w, 7 * 16)
            pe.transpose(setup[:, 0:P], w_raw[:, :], k.ident[:, :])
            pe.matmul(setup[:, 128:130], w_raw[:, :], a_cols[:, :], start=True, stop=True)
            pe.wait_ge(s_wide, 1)
            pe.matmul(setup[:, 136:138], b_wide[:, :], a_cols[:, :], start=True, stop=True).then_inc(s_setup, 1)
            pe.wait_ge(s_ext, 1)
            for u in range(U):
                pe.transpose(turned[u][:, 0:P], w_raw[:, :], k.ident[:, :]).then_inc(s_turned, 1)
                pe.matmul(prod[u][:, 0, 0:1], w_raw[:, :], a_cols[:, 0:1], start=True, stop=True).then_inc(s_prod, 1)
            with pe.Fori(0, NG // U) as i:
                for u in range(U):
                    pe.wait_ge(s_x[u], i * 16 + 16)
                    pe.wait_ge(s_xt, i * U + u)
                    for j in range(J):
                        last = pe.transpose(turned[u][:, j * P:(j + 1) * P], x[u][:, j, 0:D], k.ident[:, :])
                    last.then_inc(s_turned, 1)
                    pe.wait_ge(s_xt, i * U + u + 1)
                    pe.wait_ge(s_h, i * U + u + 1)
                    for j in range(J):
                        last = pe.matmul(prod[u][:, j, 0:K], xt[u][:, j * P:(j + 1) * P], w_ext[:, :],
                                         start=True, stop=True)
                    last.then_inc(s_prod, 1)

        @block.vector
        def _(dve):
            dve.wait_ge(s_w, 7 * 16)
            dve.tensor_scalar(b_wide[:, :], k.ones[:, 0:P], b_col[:, 0:1], None, ALU.mult).then_inc(s_wide, 1)
            dve.wait_ge(s_setup, 1)
            dve.tensor_copy(w_ext[:, :], setup[:, 0:K])
            dve.tensor_tensor(bias[:, D:K], setup[:, 136:138], a_bias[:, :], ALU.add).then_inc(s_ext, 1)
            for u in range(U):
                dve.memset(h[u][:, 0, 0:1], 0.0).then_inc(s_h, 1)
                dve.memset(x[u][:, :, D:k.XW], 0.0).then_inc(s_clear, 1)
            dve.wait_ge(s_ext, 1)
            dve.wait_ge(s_clear, U)

            def step(i, u):
                    t = (i * U + u) * J
                    dve.tensor_copy(x[u][:, :, D], k.degree[0][:, bass.ds(t, J)])
                    dve.tensor_copy(x[u][:, :, D + 1], k.row_s[:, bass.ds(t, J)])
                    dve.tensor_copy(to[u][:, :], k.row_d[:, bass.ds(t, J)]).then_inc(s_tag, 1)
                    dve.wait_ge(s_prod, i * U + u + 1 + U)
                    dve.tensor_tensor(h[u][:, :, :], prod[u][:, :, 0:K], bias[:, :].unsqueeze(1).to_broadcast([P, J, K]),
                                      ALU.add).then_inc(s_h, 1)
                    dve.wait_ge(s_h, i * U + u + 1 + U)
                    dve.tensor_copy(k.score[:, :, bass.ds(t, J)], h[u][:, :, D:K].rearrange("p j s -> p s j"))

            for u in range(U):
                step(0, u)
            with dve.Fori(1, NG // U) as i:
                for u in range(U):
                    dve.wait_ge(s_out[u], i * 16)
                    dve.wait_ge(s_sent[u], i * 16 * J)
                    step(i, u)


def lay_out_edges(nc, k):
    by_src = sbuf(nc, "by_src", [P, NT, 4], I32)
    by_dst = sbuf(nc, "by_dst", [P, NT, 4], I32)
    s_tab = sem(nc, "s_tab")
    s_put = sem(nc, "s_put")
    s_fill = [sem(nc, f"s_fill{q}") for q in range(2)]
    with nc.Block() as block:
        @block.vector
        def _(dve):
            dve.tensor_copy(by_src[:, :, 0], k.row_d[:, :])
            dve.tensor_scalar(by_src[:, :, 1], k.lane[1][:, :], 0, None, ALU.bitwise_or)
            dve.tensor_copy(by_src[:, :, 2].bitcast(F32), k.column[1][:, :])
            dve.tensor_copy(by_src[:, :, 3].bitcast(F32), k.score[:, 0, :])
            dve.tensor_scalar(by_dst[:, :, 0], k.lane[0][:, :], 0, None, ALU.bitwise_or)
            dve.tensor_copy(by_dst[:, :, 1].bitcast(F32), k.column[0][:, :])
            dve.tensor_copy(by_dst[:, :, 2].bitcast(F32), k.score[:, 1, :])
            dve.memset(by_dst[:, :, 3], 0).then_inc(s_tab, 1)

        @block.sync
        def _(sp):
            sp.wait_ge(s_tab, 1)
            sp.dma_start(k.by_src.rearrange("(h p) w -> p h w", p=P), by_src[:, :, :]).then_inc(s_put, 16)
            sp.dma_start(k.by_dst.rearrange("(h p) w -> p h w", p=P), by_dst[:, :, :]).then_inc(s_put, 16)
            for q, table, w in ((0, k.in_edges, IN_WORDS), (1, k.out_edges, OUT_WORDS)):
                items = sp.value_load(k.start[q][0:1, NG:NG + 1], min_val=NG, max_val=MAX_ITEMS) + SPARE
                view = table.rearrange("(p c) w -> p (c w)", p=P)
                with sp.Fori(0, items * J, FILL) as c:
                    sp.dma_start(view[:, bass.ds(c * w, FILL * w)], k.zeros[:, 0:FILL * w].bitcast(I32)).then_inc(s_fill[q], 16)
                steps = sp.snap((items * J + (FILL - 1)) // FILL)
                stand(sp, s_fill[q], steps * 16, k.held)
            sp.wait_ge(s_put, 32)
    T = J
    NBAT = NT // T
    U = 2
    src_of = [sbuf(nc, f"src_of{u}", [P, T], U32) for u in range(U)]
    dst_of = [sbuf(nc, f"dst_of{u}", [P, T], U32) for u in range(U)]
    from_src = [sbuf(nc, f"from_src{u}", [P, T, 4], I32) for u in range(U)]
    from_dst = [sbuf(nc, f"from_dst{u}", [P, T, 4], I32) for u in range(U)]
    col_f = [sbuf(nc, f"col_f{u}", [P, 2, T], F32) for u in range(U)]
    col_i = [sbuf(nc, f"col_i{u}", [P, 2, T], I32) for u in range(U)]
    slot = [sbuf(nc, f"slot{u}", [P, 2, T], I32) for u in range(U)]
    raw_score = [sbuf(nc, f"raw_score{u}", [P, T], F32) for u in range(U)]
    in_pay = [sbuf(nc, f"in_pay{u}", [P, T, IN_WORDS], I32) for u in range(U)]
    out_pay = [sbuf(nc, f"out_pay{u}", [P, T, OUT_WORDS], I32) for u in range(U)]
    s_index = sem(nc, "s_index")
    s_got = [sem(nc, f"s_got{u}") for u in range(U)]
    s_step = sem(nc, "s_step")
    s_slot = sem(nc, "s_slot")
    s_laid = [sem(nc, f"s_laid{u}") for u in range(U)]
    STEPS = 10
    with nc.Block() as block:
        @block.vector
        def _(dve):
            def indices(u, b):
                dve.tensor_copy(src_of[u][:, :], k.key[1][:, bass.ds(b * T, T)])
                dve.tensor_copy(dst_of[u][:, :], k.key[0][:, bass.ds(b * T, T)]).then_inc(s_index, 1)

            def slots(u, i):
                b = i * U + u
                cols = bass.ds(b * T, T)
                dve.wait_ge(s_got[u], i * 32 * T + 32 * T)
                c = Chain(dve, s_step, b * STEPS)
                c(dve.scalar_tensor_tensor(out=col_f[u][:, 0, :], in0=k.rank[0][:, cols], scalar=float(J),
                                           in1=from_dst[u][:, :, 1].bitcast(F32), op0=ALU.mult, op1=ALU.add))
                c(dve.scalar_tensor_tensor(out=col_f[u][:, 1, :], in0=k.rank[1][:, cols], scalar=float(J),
                                           in1=from_src[u][:, :, 2].bitcast(F32), op0=ALU.mult, op1=ALU.add))
                c(dve.tensor_tensor(raw_score[u][:, :], from_src[u][:, :, 3].bitcast(F32), from_dst[u][:, :, 2].bitcast(F32), ALU.add))
                c(dve.tensor_scalar(out_pay[u][:, :, 0], dst_of[u][:, :], 1.0, None, ALU.add))
                c.wait()
                c(dve.tensor_copy(col_i[u][:, :, :], col_f[u][:, :, :]))
                c(dve.scalar_tensor_tensor(out=out_pay[u][:, :, 1].bitcast(F32), in0=raw_score[u][:, :], scalar=0.01,
                                           in1=raw_score[u][:, :], op0=ALU.mult, op1=ALU.max))
                c(dve.tensor_scalar(in_pay[u][:, :, 0], from_src[u][:, :, 0], 0, None,
                                    ALU.bitwise_or))
                c.wait()
                c(dve.tensor_tensor(slot[u][:, 0, :], col_i[u][:, 0, :], from_dst[u][:, :, 0],
                                    ALU.bitwise_or))
                c(dve.tensor_tensor(slot[u][:, 1, :], col_i[u][:, 1, :], from_src[u][:, :, 1],
                                    ALU.bitwise_or))
                c(dve.tensor_copy(in_pay[u][:, :, 1].bitcast(F32), k.weight[:, cols]))
                c.wait()
                dve.tensor_tensor(slot[u][:, :, :], slot[u][:, :, :],
                                  k.past[:, cols].unsqueeze(1).to_broadcast([P, 2, T]), ALU.bitwise_or
                                  ).then_inc(s_slot, 1)

            indices(0, 0)
            for u in range(U):
                indices((u + 1) % U, u + 1)
                slots(u, 0)
            with dve.Fori(1, NBAT // U) as i:
                for u in range(U):
                    indices((u + 1) % U, i * U + u + 1)
                    dve.wait_ge(s_laid[u], i * 32 * T)
                    slots(u, i)

        @block.gpsimd
        def _(pool):
            def gather(u, b):
                stand(pool, s_index, b + 1, k.held)
                for t in range(T):
                    pool.indirect_dma_start(from_src[u][:, t, :], None, k.by_src[:, :],
                                            bass.IndirectOffsetOnAxis(ap=src_of[u][:, t:t + 1], axis=0)
                                            ).then_inc(s_got[u], 16)
                    pool.indirect_dma_start(from_dst[u][:, t, :], None, k.by_dst[:, :],
                                            bass.IndirectOffsetOnAxis(ap=dst_of[u][:, t:t + 1], axis=0)
                                            ).then_inc(s_got[u], 16)

            def scatter(u, b):
                    stand(pool, s_slot, b + 1, k.held)
                    for t in range(T):
                        for q, pay, table in ((0, in_pay, k.in_edges), (1, out_pay, k.out_edges)):
                            pool.indirect_dma_start(
                                table[:, :], bass.IndirectOffsetOnAxis(ap=slot[u][:, q, t:t + 1].bitcast(U32), axis=0),
                                pay[u][:, t, :], None, bounds_check=P * COLS - 1, oob_is_err=False
                                ).then_inc(s_laid[u], 16)

            gather(0, 0)
            gather(1, 1)
            scatter(0, 0)
            with pool.Fori(1, NBAT - 1, U) as b:
                for u in range(U):
                    gather((u + U) % U, b + u + 1)
                    scatter((u + 1) % U, b + u)
            scatter((NBAT - 1) % U, NBAT - 1)
            for u in range(U):
                pool.wait_ge(s_laid[u], 32 * T * (NBAT // U))


def cut_off(nc, k):
    edges = sbuf(nc, "edges", [P, FILL, IN_WORDS], I32)
    angle, within, cosine, factor, turns, back = [
        sbuf(nc, n, [P, FILL], F32) for n in ("angle", "within", "cosine", "factor", "turns", "back")]
    turns_i = sbuf(nc, "turns_i", [P, FILL], I32)
    quarter = sbuf(nc, "quarter", [P, 1], F32)
    s_edges, s_angle, s_cosine, s_factor, s_kept, s_step = [
        sem(nc, n) for n in ("s_edges", "s_angle", "s_cosine", "s_factor", "s_kept", "s_step")]
    with nc.Block() as block:
        @block.sync
        def _(sp):
            items = sp.value_load(k.start[0][0:1, NG:NG + 1], min_val=NG, max_val=MAX_ITEMS) + SPARE
            steps = sp.snap((items * J + (FILL - 1)) // FILL)
            view = k.in_edges.rearrange("(p c) w -> p (c w)", p=P)
            out = k.cutoffs.rearrange("(p c) w -> p (c w)", p=P)
            with sp.Fori(0, steps) as n:
                sp.dma_start(edges[:, :, :].rearrange("p c w -> p (c w)"),
                             view[:, bass.ds(n * FILL * IN_WORDS, FILL * IN_WORDS)]).then_inc(s_edges, 16)
                stand(sp, s_factor, n + 1, k.held)
                sp.dma_start(out[:, bass.ds(n * FILL, FILL)], factor[:, :]).then_inc(s_kept, 16)
                stand(sp, s_kept, n * 16 + 16, k.held)

        @block.vector
        def _(dve):
            items = dve.value_load(k.start[0][0:1, NG:NG + 1], min_val=NG, max_val=MAX_ITEMS) + SPARE
            steps = dve.snap((items * J + (FILL - 1)) // FILL)
            dve.memset(quarter[:, :], np.pi / 2).then_inc(s_angle, 1)
            with dve.Fori(0, steps) as n:
                w = edges[:, :, 1].bitcast(F32)
                dve.wait_ge(s_edges, n * 16 + 16)
                c = Chain(dve, s_step, n * 8)
                c(dve.tensor_scalar(within[:, :], w, CUTOFF, 0.5, ALU.is_lt, ALU.mult))
                c(dve.tensor_scalar(back[:, :], w, CUTOFF, None, ALU.min))
                c.wait()
                c(dve.tensor_scalar(turns_i[:, :], back[:, :], 0.5 / CUTOFF, None, ALU.mult))
                c.wait()
                c(dve.tensor_copy(turns[:, :], turns_i[:, :]))
                c.wait()
                c(dve.scalar_tensor_tensor(out=turns[:, :], in0=turns[:, :], scalar=-2 * CUTOFF, in1=back[:, :],
                                           op0=ALU.mult, op1=ALU.add))
                c.wait()
                c(dve.scalar_tensor_tensor(out=turns[:, :], in0=turns[:, :], scalar=-1.0, in1=turns[:, :],
                                           op0=ALU.mult, op1=ALU.max))
                c.wait()
                c(dve.tensor_scalar(back[:, :], turns[:, :], -1.0, 2 * CUTOFF, ALU.mult, ALU.add))
                c.wait()
                c(dve.tensor_tensor(angle[:, :], turns[:, :], back[:, :], ALU.min))
                c.wait()
                c.all(8)
                dve.sem_inc(s_angle, 1)
                dve.wait_ge(s_cosine, n + 1)
                dve.scalar_tensor_tensor(out=factor[:, :], in0=cosine[:, :], scalar=1.0, in1=within[:, :],
                                         op0=ALU.add, op1=ALU.mult).then_inc(s_factor, 1)

        @block.scalar
        def _(act):
            items = act.value_load(k.start[0][0:1, NG:NG + 1], min_val=NG, max_val=MAX_ITEMS) + SPARE
            steps = act.snap((items * J + (FILL - 1)) // FILL)
            with act.Fori(0, steps) as n:
                act.wait_ge(s_angle, n + 2)
                act.activation(cosine[:, :], angle[:, :], ACT.Sin, bias=quarter[:, 0:1], scale=-np.pi / CUTOFF
                               ).then_inc(s_cosine, 1)


NEG = -1e30


def bounds(eng, k, q, g):
    lo = eng.value_load(k.start[q][0:1, bass.ds(g, 1)], min_val=0, max_val=MAX_ITEMS)
    hi = eng.value_load(k.start[q][0:1, bass.ds(g + 1, 1)], min_val=1, max_val=MAX_ITEMS + 1)
    return lo, hi


def bounds_of(eng, k, i, u, ends):
    if u == 0:
        ends[:] = [eng.value_load(k.start[0][0:1, bass.ds(i * 2 + n, 1)], min_val=min(n, 1), max_val=MAX_ITEMS + n)
                   for n in range(3)]
    return ends[u], ends[u + 1]


DEPTH = 4


def feed_items(sp, k, q, loads, s_ring, s_got, s_here, s_used):
    items = sp.value_load(k.start[q][0:1, NG:NG + 1], min_val=NG, max_val=MAX_ITEMS)

    def load(i, u):
        for table, words, ring in loads:
            view = table.rearrange("(p c) w -> p (c w)", p=P)
            sp.dma_start(ring[:, u, :], view[:, bass.ds(i * J * words, J * words)]).then_inc(s_ring, 16)
        stand(sp, s_ring, i * 16 * len(loads) + 16 * len(loads), k.held)

    def block(b, first):
        for u in range(DEPTH):
            i = b * DEPTH + u
            if not (first and u == 0):
                stand(sp, s_used, i, k.held)
            load(i + 3, (u + 3) % DEPTH)
            stand(sp, s_got[u], b * 16 * J + 16 * J, k.held)
            sp.sem_inc(s_here, 1)

    for u in range(3):
        load(u, u)
    block(0, True)
    with sp.Fori(1, sp.snap((items + (DEPTH - 1)) // DEPTH)) as b:
        block(b, False)


def gather_ahead(pool, k, q, rows, ring, words, s_ring, per_ring, got, s_got, s_here, s_used):
    items = pool.value_load(k.start[q][0:1, NG:NG + 1], min_val=NG, max_val=MAX_ITEMS)

    def block(b, first):
        for u in range(DEPTH):
            i = b * DEPTH + u
            stand(pool, s_ring, i * per_ring + per_ring, k.held)
            if not first:
                stand(pool, s_here, i - DEPTH + 1, k.held)
                stand(pool, s_used, i - DEPTH + 1, k.held)
            for j in range(J):
                pool.indirect_dma_start(got[:, u, j, :], None, rows,
                                        bass.IndirectOffsetOnAxis(ap=ring[:, u, j * words:j * words + 1].bitcast(U32),
                                                                  axis=0)).then_inc(s_got[u], 16)

    block(0, True)
    blocks = pool.snap((items + (DEPTH - 1)) // DEPTH)
    with pool.Fori(1, blocks) as b:
        block(b, False)
    for u in range(DEPTH):
        stand(pool, s_got[u], blocks * (16 * J), k.held)


def attend(nc, k):
    ring = sbuf(nc, "ring", [P, DEPTH, J * OUT_WORDS], I32)
    got = sbuf(nc, "got", [P, DEPTH, J, D], F32)
    part = sbuf(nc, "part", [P, J, D], F32)
    mix = sbuf(nc, "mix", [P, J, D], F32)
    out = sbuf(nc, "out", [P, J, D], F32)
    valid = sbuf(nc, "valid", [P, J], F32)
    bar = sbuf(nc, "bar", [P, J], F32)
    score = sbuf(nc, "score", [P, J], F32)
    top = sbuf(nc, "top", [P, J], F32)
    new_top = sbuf(nc, "new_top", [P, J], F32)
    drop = sbuf(nc, "drop", [P, 2 * J], F32)
    factor = sbuf(nc, "factor", [P, 2 * J], F32)
    total = sbuf(nc, "total", [P, J], F32)
    s_ring = sem(nc, "s_ring")
    s_got = [sem(nc, f"s_got{j}") for j in range(DEPTH)]
    s_here, s_part, s_used, s_drop, s_factor, s_step, s_out, s_kept = [
        sem(nc, n) for n in ("s_here", "s_part", "s_used", "s_drop", "s_factor", "s_step", "s_out", "s_kept")]
    PER_ITEM, PER_GROUP = 14, 5
    with nc.Block() as block:
        @block.sync
        def _(sp):
            feed_items(sp, k, 1, ((k.out_edges, OUT_WORDS, ring),), s_ring, s_got, s_here, s_used)

        @block.gpsimd
        def _(pool):
            gather_ahead(pool, k, 1, k.h0[:, :], ring, OUT_WORDS, s_ring, 16, got, s_got, s_here, s_used)

        @block.scalar
        def _(act):
            act.preload_act_table_set("natural_log_exp_and_others")

            def group(g):
                lo, hi = bounds(act, k, 1, g)
                with act.If(lo < hi), act.Fori(lo, hi) as i:
                    act.wait_ge(s_drop, i + 1)
                    act.activation(factor[:, :], drop[:, :], ACT.Exp).then_inc(s_factor, 1)
                stand(act, s_out, g + 1, k.held)
                act.dma_start(k.mix[bass.ds(g * G + 1, G), :].rearrange("(p j) d -> p (j d)", j=J),
                              out[:, :, :].rearrange("p j d -> p (j d)")).then_inc(s_kept, 16)

            with act.Fori(0, NG) as g:
                group(g)
            act.wait_ge(s_kept, 16 * NG)

        @block.vector
        def _(dve):
            def item(i, g):
                c = Chain(dve, s_step, i * PER_ITEM + g * PER_GROUP + 3)
                c.wait()
                half = ring[:, bass.ds(i % DEPTH, 1), :].rearrange("p a (j w) -> p (a j) w", w=OUT_WORDS)
                dve.wait_ge(s_ring, i * 16 + 16)
                c(dve.tensor_scalar(valid[:, :], half[:, :, 0], 0.0, None, ALU.not_equal))
                c.wait()
                c(dve.tensor_scalar(bar[:, :], valid[:, :], -NEG, NEG, ALU.mult, ALU.add))
                c.wait()
                c(dve.tensor_tensor(score[:, :], bar[:, :], half[:, :, 1].bitcast(F32), ALU.add))
                c.wait()
                c(dve.tensor_tensor(new_top[:, :], top[:, :], score[:, :], ALU.max))
                c.wait()
                c(dve.tensor_tensor(drop[:, 0:J], top[:, :], new_top[:, :], ALU.subtract))
                c(dve.tensor_tensor(drop[:, J:2 * J], score[:, :], new_top[:, :], ALU.subtract))
                c.wait()
                c(dve.tensor_copy(top[:, :], new_top[:, :]))
                dve.sem_inc(s_drop, 1)
                dve.wait_ge(s_factor, i + 1)
                c(dve.tensor_tensor(total[:, :], total[:, :], factor[:, 0:J], ALU.mult))
                c(dve.tensor_tensor(score[:, :], factor[:, J:2 * J], valid[:, :], ALU.mult))
                c.wait()
                c(dve.tensor_tensor(total[:, :], total[:, :], score[:, :], ALU.add))
                rows = got[:, bass.ds(i % DEPTH, 1), :, :].rearrange("p a j d -> p (a j) d")
                c.wait()
                dve.wait_ge(s_here, i + 1)
                for j in range(J):
                    dve.tensor_scalar(part[:, j, :], rows[:, j, :], score[:, j:j + 1], None, ALU.mult).then_inc(s_part, 1)
                dve.wait_ge(s_part, i * J + J)
                dve.sem_inc(s_used, 1)
                for j in range(J):
                    c(dve.scalar_tensor_tensor(out=mix[:, j, :], in0=mix[:, j, :], scalar=factor[:, j:j + 1],
                                               in1=part[:, j, :], op0=ALU.mult, op1=ALU.add))

            def group(g, first):
                lo, hi = bounds(dve, k, 1, g)
                with dve.If(lo < hi), dve.Fori(lo, hi) as i:
                    item(i, g)
                c = Chain(dve, s_step, hi * PER_ITEM + g * PER_GROUP + 3)
                c.wait()
                c(dve.tensor_scalar(total[:, :], total[:, :], 1e-30, None, ALU.max))
                c.wait()
                c(dve.reciprocal(total[:, :], total[:, :]))
                c.wait()
                if not first:
                    dve.wait_ge(s_kept, g * 16)
                for j in range(J):
                    last = dve.tensor_scalar(out[:, j, :], mix[:, j, :], total[:, j:j + 1], None, ALU.mult)
                last.then_inc(s_out, 1)
                dve.wait_ge(s_out, g + 1)
                c(dve.memset(mix[:, :, :], 0.0))
                c(dve.memset(total[:, :], 0.0))
                c(dve.memset(top[:, :], NEG))

            dve.memset(mix[:, :, :], 0.0).then_inc(s_step, 1)
            dve.memset(total[:, :], 0.0).then_inc(s_step, 1)
            dve.memset(top[:, :], NEG).then_inc(s_step, 1)
            group(0, True)
            with dve.Fori(1, NG) as g:
                group(g, False)
            dve.sem_inc(s_used, DEPTH)

def own_rows(table, g):
    return table[bass.ds(g * G + 1, G), :].rearrange("(p j) d -> p (j d)", j=J)


def flat(t):
    return t.rearrange("p j d -> p (j d)")


def spread_stats(dve, k, c, y, stats, moments):
    for j in range(J):
        c(dve.bn_stats(stats[:, j, :], y[:, j, :]))
    stand(dve, c.sem, c.base + c.n, k.held)
    for j in range(J):
        c(dve.bn_aggr(moments[:, j, :], stats[:, j, :]))
    c.wait()


def inverse_spread(act, k, moments, log_var, spread, s_log, n):
    act.activation(log_var[:, :], moments[:, :, 1], ACT.Ln, bias=k.eps[:, 0:1]).then_inc(s_log, 1)
    act.wait_ge(s_log, n + 1)
    return act.activation(spread[:, :], log_var[:, :], ACT.Exp, scale=-0.5)


def join_attention(nc, k):
    U = 7
    assert NG % U == 0
    x = [sbuf(nc, f"x{u}", [P, J, XW], F32) for u in range(U)]
    to = [sbuf(nc, f"to{u}", [P, J], U32) for u in range(U)]
    mix = [sbuf(nc, f"mix{u}", [P, J, D], F32) for u in range(U)]
    y = [sbuf(nc, f"y{u}", [P, J, D], F32) for u in range(U)]
    stats = sbuf(nc, "stats", [P, J, 6], F32)
    moments = sbuf(nc, "moments", [P, J, 2], F32)
    log_var = sbuf(nc, "log_var", [P, J], F32)
    spread = sbuf(nc, "spread", [P, J], F32)
    s_x = [sem(nc, f"s_x{u}") for u in range(U)]
    s_mix = [sem(nc, f"s_mix{u}") for u in range(U)]
    s_kept = [sem(nc, f"s_kept{u}") for u in range(U)]
    s_tag, s_step, s_mom, s_log, s_spread, s_y = [
        sem(nc, n) for n in ("s_tag", "s_step", "s_mom", "s_log", "s_spread", "s_y")]
    PER = 13
    with nc.Block() as block:
        @block.sync
        def _(sp):
            def load(b, u):
                sp.dma_start(flat(x[u][:, :, :]), own_rows(k.xd, b)).then_inc(s_x[u], 16)

            for u in range(U):
                load(u, u)
            with sp.Fori(1, NG // U) as i:
                for u in range(U):
                    stand(sp, s_y, i * U + u - U + 1, k.held)
                    load(i * U + u, u)

        @block.gpsimd
        def _(pool):
            with pool.Fori(0, NG // U) as i:
                for u in range(U):
                    stand(pool, s_tag, i * U + u + 1, k.held)
                    for j in range(J):
                        pool.indirect_dma_start(mix[u][:, j, :], None, k.mix[:, :],
                                                bass.IndirectOffsetOnAxis(ap=to[u][:, j:j + 1], axis=0)
                                                ).then_inc(s_mix[u], 16)
            for u in range(U):
                pool.wait_ge(s_mix[u], 16 * J * NG // U)

        @block.scalar
        def _(act):
            act.preload_act_table_set("natural_log_exp_and_others")
            with act.Fori(0, NG // U) as i:
                for u in range(U):
                    b = i * U + u
                    act.wait_ge(s_mom, b + 1)
                    inverse_spread(act, k, moments, log_var, spread, s_log, b).then_inc(s_spread, 1)
                    stand(act, s_y, b + 1, k.held)
                    act.dma_start(own_rows(k.ya, b), flat(y[u][:, :, :])).then_inc(s_kept[u], 16)
            for u in range(U):
                act.wait_ge(s_kept[u], 16 * NG // U)

        @block.vector
        def _(dve):
            def front(i, u):
                b = i * U + u
                cols = bass.ds(b * J, J)
                dve.wait_ge(s_x[u], i * 16 + 16)
                dve.tensor_copy(k.in_degree[:, cols], x[u][:, :, D])
                dve.tensor_copy(to[u][:, :], x[u][:, :, D + 1]).then_inc(s_tag, 1)

            def back(i, u, first):
                b = i * U + u
                c = Chain(dve, s_step, b * PER)
                dve.wait_ge(s_mix[u], i * 16 * J + 16 * J)
                if not first:
                    dve.wait_ge(s_kept[u], i * 16)
                c(dve.tensor_tensor(y[u][:, :, :], x[u][:, :, 0:D], mix[u][:, :, :], ALU.add))
                c.wait()
                spread_stats(dve, k, c, y[u], stats, moments)
                dve.sem_inc(s_mom, 1)
                dve.wait_ge(s_spread, b + 1)
                for j in range(J):
                    c(dve.tensor_scalar(y[u][:, j, :], y[u][:, j, :], moments[:, j, 0:1], spread[:, j:j + 1],
                                        ALU.subtract, ALU.mult))
                c.wait()
                dve.sem_inc(s_y, 1)
                c.all(PER)

            def groups(i, first, last):
                for u in range(U):
                    if u + 1 < U:
                        front(i, u + 1)
                    elif not last:
                        front(i + 1, 0)
                    back(i, u, first)

            front(0, 0)
            groups(0, True, False)
            with dve.Fori(1, NG // U - 1) as i:
                groups(i, False, False)
            groups(NG // U - 1, False, True)


def hyperbolic(nc, k):
    EPS = 1e-7
    ring = sbuf(nc, "ring", [P, DEPTH, J * IN_WORDS], I32)
    got = sbuf(nc, "got", [P, DEPTH, J, D], F32)
    own = sbuf(nc, "own", [P, 2, J, D], F32)
    msg = sbuf(nc, "msg", [P, J, D], F32)
    part = sbuf(nc, "part", [P, J, D], F32)
    total = sbuf(nc, "total", [P, J, D], F32)
    waste = sbuf(nc, "waste", [P, J, D], F32)
    junk = [sbuf(nc, f"junk{n}", [P, J, D], F32) for n in range(4)]
    y = sbuf(nc, "y", [P, J, D], F32)
    stats = sbuf(nc, "stats", [P, J, 6], F32)
    moments = sbuf(nc, "moments", [P, J, 2], F32)
    log_var = sbuf(nc, "log_var", [P, J], F32)
    spread = sbuf(nc, "spread", [P, J], F32)
    col = lambda name: sbuf(nc, name, [P, J], F32)
    own_sqs = sbuf(nc, "own_sqs", [P, 2, J], F32)
    got_sq, msg_sq, total_sq, got_own, total_msg, valid = [
        col(n) for n in ("got_sq", "msg_sq", "total_sq", "got_own", "total_msg", "valid")]
    lin, den, inv, num, fa, fb = [col(n) for n in ("lin", "den", "inv", "num", "fa", "fb")]
    lin2, den2, inv2, num2, fc, fd = [col(n) for n in ("lin2", "den2", "inv2", "num2", "fc", "fd")]
    own_total, size, log_size, root, log_up, log_down, arc, power, tanh, share, large = [
        col(n) for n in ("own_total", "size", "log_size", "root", "log_up", "log_down", "arc", "power", "tanh",
                         "share", "large")]
    s_ring = sem(nc, "s_ring")
    s_got = [sem(nc, f"s_got{j}") for j in range(DEPTH)]
    s_here, s_part = [sem(nc, n) for n in ("s_here", "s_part")]
    (s_used, s_own, s_own_sq, s_got_sq, s_total_sq, s_msg, s_msg_sq, s_fold, s_end_sq, s_size, s_root, s_ball, s_logs,
     s_arc, s_power, s_mom, s_log, s_spread, s_y, s_kept, s_step) = [sem(nc, n) for n in (
         "s_used", "s_own", "s_own_sq", "s_got_sq", "s_total_sq", "s_msg", "s_msg_sq", "s_fold", "s_end_sq", "s_size",
         "s_root", "s_ball", "s_logs", "s_arc", "s_power", "s_mom", "s_log", "s_spread", "s_y", "s_kept", "s_step")]
    PER_ITEM, PER_GROUP = PER_HYPERBOLIC
    with nc.Block() as block:
        @block.sync
        def _(sp):
            feed_items(sp, k, 0, ((k.in_edges, IN_WORDS, ring),), s_ring, s_got, s_here, s_used)

        @block.gpsimd
        def _(pool):
            gather_ahead(pool, k, 0, k.ya[:, :], ring, IN_WORDS, s_ring, 16, got, s_got, s_here, s_used)

        @block.scalar
        def _(act):
            act.preload_act_table_set("natural_log_exp_and_others")

            def squares(of, to, n):
                for j in range(J):
                    last = act.activation(junk[n][:, j, :], of(j), ACT.Square, accum_out=to[:, j:j + 1])
                return last

            def load(g, half):
                act.dma_start(own[:, half, :, :].rearrange("p a j d -> p (a j d)"), own_rows(k.ya, g)
                              ).then_inc(s_own, 16)

            def item(i, g):
                act.wait_ge(s_here, i + 1)
                rows = got[:, bass.ds(i % DEPTH, 1), :, :].rearrange("p a j d -> p (a j) d")
                squares(lambda j: rows[:, j, :], got_sq, 3).then_inc(s_got_sq, 1)
                act.wait_ge(s_fold, i + g + 1)
                squares(lambda j: total[:, j, :], total_sq, 1).then_inc(s_total_sq, 1)
                act.wait_ge(s_msg, i + 1)
                squares(lambda j: msg[:, j, :], msg_sq, 2).then_inc(s_msg_sq, 1)

            def own_squares(g):
                stand(act, s_own, g * 16 + 16, k.held)
                mine = own[:, bass.ds(g % 2, 1), :, :].rearrange("p a j d -> p (a j) d")
                squares(lambda j: mine[:, j, :], own_sqs[:, bass.ds(g % 2, 1), :].rearrange("p a j -> p (a j)"), 0
                        ).then_inc(s_own_sq, 1)

            def group(g, later):
                lo, hi = bounds(act, k, 0, g)
                with act.If(lo < hi), act.Fori(lo, hi) as i:
                    item(i, g)
                act.wait_ge(s_end_sq, g + 1)
                squares(lambda j: total[:, j, :], total_sq, 1).then_inc(s_size, 1)
                act.wait_ge(s_root, g * 2 + 1)
                act.activation(log_size[:, :], size[:, :], ACT.Ln).then_inc(s_log, 1)
                act.wait_ge(s_log, g * 2 + 1)
                act.activation(root[:, :], log_size[:, :], ACT.Exp, scale=0.5).then_inc(s_ball, 1)
                act.wait_ge(s_root, g * 2 + 2)
                act.activation(log_up[:, :], root[:, :], ACT.Ln, bias=1.0)
                act.activation(log_down[:, :], root[:, :], ACT.Ln, bias=1.0, scale=-1.0).then_inc(s_logs, 1)
                act.wait_ge(s_arc, g + 1)
                act.activation(power[:, :], arc[:, :], ACT.Exp).then_inc(s_power, 1)
                if later > 0:
                    own_squares(g + 1)
                act.wait_ge(s_mom, g + 1)
                inverse_spread(act, k, moments, log_var, spread, s_log, g * 2 + 1).then_inc(s_spread, 1)
                stand(act, s_y, g + 1, k.held)
                act.dma_start(own_rows(k.yb, g), flat(y[:, :, :])).then_inc(s_kept, 16)
                if later > 1:
                    load(g + 2, bass.ds(g % 2, 1))

            load(0, slice(0, 1))
            own_squares(0)
            load(1, slice(1, 2))
            group(0, 2)
            with act.Fori(1, NG - 2) as g:
                group(g, 2)
            group(NG - 2, 1)
            group(NG - 1, 0)
            act.wait_ge(s_kept, 16 * NG)

        @block.vector
        def _(dve):
            def item(i, g, mine, own_sq):
                c = Chain(dve, s_step, i * PER_ITEM + g * PER_GROUP)
                half = ring[:, bass.ds(i % DEPTH, 1), :].rearrange("p a (j w) -> p (a j) w", w=IN_WORDS)
                rows = got[:, bass.ds(i % DEPTH, 1), :, :].rearrange("p a j d -> p (a j) d")
                c.wait()
                dve.wait_ge(s_here, i + 1)
                for j in range(J):
                    c(dve.scalar_tensor_tensor(out=waste[:, j, :], in0=rows[:, j, :], scalar=1.0, in1=mine[:, j, :],
                                               op0=ALU.mult, op1=ALU.mult, accum_out=got_own[:, j:j + 1]))
                c.wait()
                dve.wait_ge(s_ring, i * 16 + 16)
                c(dve.tensor_scalar(valid[:, :], half[:, :, 0], 0.0, None, ALU.not_equal))
                c(dve.tensor_scalar(lin[:, :], got_own[:, :], -2.0, 1.0, ALU.mult, ALU.add))
                dve.wait_ge(s_got_sq, i + 1)
                c(dve.tensor_tensor(den[:, :], got_sq[:, :], own_sq, ALU.mult))
                c.wait()
                c(dve.tensor_tensor(den[:, :], den[:, :], lin[:, :], ALU.add))
                c(dve.tensor_tensor(num[:, :], lin[:, :], own_sq, ALU.add))
                c.wait()
                c(dve.tensor_scalar(den[:, :], den[:, :], EPS, None, ALU.max))
                c.wait()
                c(dve.reciprocal(inv[:, :], den[:, :]))
                c.wait()
                c(dve.tensor_tensor(inv[:, :], inv[:, :], valid[:, :], ALU.mult))
                c.wait()
                c(dve.tensor_tensor(fa[:, :], num[:, :], inv[:, :], ALU.mult))
                c(dve.scalar_tensor_tensor(out=fb[:, :], in0=got_sq[:, :], scalar=-1.0, in1=inv[:, :],
                                           op0=ALU.add, op1=ALU.mult))
                c.wait()
                for j in range(J):
                    dve.tensor_scalar(part[:, j, :], rows[:, j, :], fa[:, j:j + 1], None, ALU.mult).then_inc(s_part, 1)
                dve.wait_ge(s_part, i * J + J)
                dve.sem_inc(s_used, 1)
                for j in range(J):
                    c(dve.scalar_tensor_tensor(out=msg[:, j, :], in0=mine[:, j, :], scalar=fb[:, j:j + 1],
                                               in1=part[:, j, :], op0=ALU.mult, op1=ALU.add))
                c.wait()
                dve.sem_inc(s_msg, 1)
                for j in range(J):
                    c(dve.scalar_tensor_tensor(out=waste[:, j, :], in0=total[:, j, :], scalar=1.0, in1=msg[:, j, :],
                                               op0=ALU.mult, op1=ALU.mult, accum_out=total_msg[:, j:j + 1]))
                c.wait()
                c(dve.tensor_scalar(lin2[:, :], total_msg[:, :], 2.0, 1.0, ALU.mult, ALU.add))
                dve.wait_ge(s_msg_sq, i + 1)
                c(dve.tensor_tensor(den2[:, :], total_sq[:, :], msg_sq[:, :], ALU.mult))
                c.wait()
                c(dve.tensor_tensor(den2[:, :], den2[:, :], lin2[:, :], ALU.add))
                c(dve.tensor_tensor(num2[:, :], lin2[:, :], msg_sq[:, :], ALU.add))
                c.wait()
                c(dve.tensor_scalar(den2[:, :], den2[:, :], EPS, None, ALU.max))
                c.wait()
                c(dve.reciprocal(inv2[:, :], den2[:, :]))
                c.wait()
                c(dve.tensor_tensor(fc[:, :], num2[:, :], inv2[:, :], ALU.mult))
                c(dve.tensor_scalar(fd[:, :], total_sq[:, :], -1.0, 1.0, ALU.mult, ALU.add))
                c.wait()
                c(dve.tensor_tensor(fd[:, :], fd[:, :], inv2[:, :], ALU.mult))
                c.wait()
                for j in range(J):
                    c(dve.tensor_scalar(part[:, j, :], msg[:, j, :], fd[:, j:j + 1], None, ALU.mult))
                c.wait()
                for j in range(J):
                    c(dve.scalar_tensor_tensor(out=total[:, j, :], in0=total[:, j, :], scalar=fc[:, j:j + 1],
                                               in1=part[:, j, :], op0=ALU.mult, op1=ALU.add))
                c.wait()
                dve.sem_inc(s_fold, 1)
                c.all(PER_ITEM)

            def group(g, first):
                mine = own[:, bass.ds(g % 2, 1), :, :].rearrange("p a j d -> p (a j) d")
                own_sq = own_sqs[:, bass.ds(g % 2, 1), :].rearrange("p a j -> p (a j)")
                lo, hi = bounds(dve, k, 0, g)
                stand(dve, s_own_sq, g + 1, k.held)
                with dve.If(lo < hi), dve.Fori(lo, hi) as i:
                    item(i, g, mine, own_sq)
                c = Chain(dve, s_step, hi * PER_ITEM + g * PER_GROUP)
                c.wait()
                dve.sem_inc(s_end_sq, 1)
                for j in range(J):
                    c(dve.scalar_tensor_tensor(out=waste[:, j, :], in0=total[:, j, :], scalar=1.0, in1=mine[:, j, :],
                                               op0=ALU.mult, op1=ALU.mult, accum_out=own_total[:, j:j + 1]))
                c.wait()
                c(dve.tensor_scalar(share[:, :], k.in_degree[:, bass.ds(g * J, J)], 1.0, None, ALU.max))
                c.wait()
                c(dve.reciprocal(share[:, :], share[:, :]))
                dve.wait_ge(s_size, g + 1)
                c(dve.tensor_scalar(size[:, :], total_sq[:, :], EPS * EPS, None, ALU.max))
                c(dve.tensor_scalar(large[:, :], total_sq[:, :], EPS * EPS, None, ALU.is_gt))
                c.wait()
                dve.sem_inc(s_root, 1)
                dve.wait_ge(s_ball, g + 1)
                c(dve.tensor_scalar(root[:, :], root[:, :], EPS, 1.0 - EPS, ALU.max, ALU.min))
                c.wait()
                dve.sem_inc(s_root, 1)
                dve.wait_ge(s_logs, g + 1)
                c(dve.tensor_tensor(arc[:, :], log_up[:, :], log_down[:, :], ALU.subtract))
                c.wait()
                c(dve.tensor_tensor(arc[:, :], arc[:, :], share[:, :], ALU.mult))
                c.wait()
                dve.sem_inc(s_arc, 1)
                dve.wait_ge(s_power, g + 1)
                c(dve.scalar_tensor_tensor(out=tanh[:, :], in0=power[:, :], scalar=1.0, in1=root[:, :],
                                           op0=ALU.add, op1=ALU.mult))
                c.wait()
                c(dve.reciprocal(tanh[:, :], tanh[:, :]))
                c.wait()
                c(dve.scalar_tensor_tensor(out=tanh[:, :], in0=power[:, :], scalar=-1.0, in1=tanh[:, :],
                                           op0=ALU.add, op1=ALU.mult))
                c.wait()
                c(dve.tensor_tensor(tanh[:, :], tanh[:, :], large[:, :], ALU.mult))
                c.wait()
                c(dve.tensor_tensor(lin[:, :], tanh[:, :], own_total[:, :], ALU.mult))
                c(dve.tensor_tensor(num[:, :], tanh[:, :], tanh[:, :], ALU.mult))
                c.wait()
                c(dve.tensor_scalar(lin[:, :], lin[:, :], 2.0, 1.0, ALU.mult, ALU.add))
                c(dve.tensor_tensor(num[:, :], num[:, :], total_sq[:, :], ALU.mult))
                c.wait()
                c(dve.tensor_tensor(den[:, :], num[:, :], own_sq, ALU.mult))
                c(dve.tensor_tensor(fa[:, :], num[:, :], lin[:, :], ALU.add))
                c.wait()
                c(dve.tensor_tensor(den[:, :], den[:, :], lin[:, :], ALU.add))
                c(dve.tensor_scalar(fb[:, :], own_sq, -1.0, 1.0, ALU.mult, ALU.add))
                c.wait()
                c(dve.tensor_scalar(den[:, :], den[:, :], EPS, None, ALU.max))
                c(dve.tensor_tensor(fb[:, :], fb[:, :], tanh[:, :], ALU.mult))
                c.wait()
                c(dve.reciprocal(inv[:, :], den[:, :]))
                c.wait()
                c(dve.tensor_tensor(fb[:, :], fb[:, :], inv[:, :], ALU.mult))
                c(dve.tensor_tensor(fa[:, :], fa[:, :], inv[:, :], ALU.mult))
                c.wait()
                c(dve.tensor_scalar(fa[:, :], fa[:, :], 1.0, None, ALU.add))
                for j in range(J):
                    c(dve.tensor_scalar(part[:, j, :], total[:, j, :], fb[:, j:j + 1], None, ALU.mult))
                c.wait()
                if not first:
                    dve.wait_ge(s_kept, g * 16)
                for j in range(J):
                    c(dve.scalar_tensor_tensor(out=y[:, j, :], in0=mine[:, j, :], scalar=fa[:, j:j + 1],
                                               in1=part[:, j, :], op0=ALU.mult, op1=ALU.add))
                c(dve.memset(total[:, :, :], 0.0))
                c.wait()
                dve.sem_inc(s_fold, 1)
                spread_stats(dve, k, c, y, stats, moments)
                dve.sem_inc(s_mom, 1)
                dve.wait_ge(s_spread, g + 1)
                for j in range(J):
                    c(dve.tensor_scalar(y[:, j, :], y[:, j, :], moments[:, j, 0:1], spread[:, j:j + 1],
                                        ALU.subtract, ALU.mult))
                c.wait()
                dve.sem_inc(s_y, 1)
                c.all(PER_GROUP)

            dve.memset(total[:, :, :], 0.0).then_inc(s_fold, 1)
            dve.wait_ge(s_fold, 1)
            group(0, True)
            with dve.Fori(1, NG) as g:
                group(g, False)
            dve.sem_inc(s_used, DEPTH)


PER_HYPERBOLIC = 39, 50
HALF = NG // 2


def over_groups(eng, body):
    for i in range(2):
        for u in range(2):
            body(i, u)
    with eng.Fori(2, HALF - 1) as i:
        for u in range(2):
            body(i, u)
    for u in range(2):
        body(HALF - 1, u)


def before(i, u):
    return (i - 1, 1) if u == 0 else (i, 0)


def third_before(i, u):
    return (i - 2, 1) if u == 0 else (i - 1, 0)


def starts(i, u, n=1):
    return isinstance(i, int) and i * 2 + u < n


def free_again(eng, sem_, i, held):
    if not (isinstance(i, int) and i == 0):
        stand(eng, sem_, i * 16, held)


def mean_layer(nc, k, n, src, dst):
    final = n == 2
    W, b = k.mean_w[n], k.mean_b[n]
    ring = sbuf(nc, "ring", [P, DEPTH, J * IN_WORDS], I32)
    got = sbuf(nc, "got", [P, DEPTH, J, D], F32)
    idle = sbuf(nc, "idle", [1, 1], F32)
    pair = lambda name: [sbuf(nc, f"{name}{u}", [P, J, D], F32) for u in range(2)]
    own, acc, own_t, acc_t, y, base, new_t, h = [
        pair(n_) for n_ in ("own", "acc", "own_t", "acc_t", "y", "base", "new_t", "h")]
    z = sbuf(nc, "z", [P, J, D], F32)
    inv = sbuf(nc, "inv", [P, J], F32)
    w_own, w_acc, w_next, bias = [sbuf(nc, n_, [P, D], F32) for n_ in ("w_own", "w_acc", "w_next", "bias")]
    stats = sbuf(nc, "stats", [P, J, 6], F32)
    moments = sbuf(nc, "moments", [P, J, 2], F32)
    log_var = sbuf(nc, "log_var", [P, J], F32)
    spread = sbuf(nc, "spread", [P, J], F32)
    own_p, acc_p, prod, new_p, h_p = [psum(nc, n_, [P, J, D], F32) for n_ in ("own_p", "acc_p", "prod", "new_p", "h_p")]
    s_ring = sem(nc, "s_ring")
    s_got = [sem(nc, f"s_got{j}") for j in range(DEPTH)]
    s_here = sem(nc, "s_here")
    s_own, s_base, s_kept_y, s_kept_h = [[sem(nc, f"{n_}{u}") for u in range(2)]
                                         for n_ in ("s_own", "s_base", "s_kept_y", "s_kept_h")]
    (s_w, s_used, s_step, s_acc, s_own_p, s_acc_p, s_own_t, s_acc_t, s_prod, s_z, s_y, s_mom, s_log, s_spread, s_new_p,
     s_new_t, s_h_p, s_h, s_end) = [sem(nc, n_) for n_ in (
         "s_w", "s_used", "s_step", "s_acc", "s_own_p", "s_acc_p", "s_own_t", "s_acc_t", "s_prod", "s_z", "s_y",
         "s_mom", "s_log", "s_spread", "s_new_p", "s_new_t", "s_h_p", "s_h", "s_end")]
    PER_ITEM = J
    FRONT = 3 + (2 + 2 * J if final else 0)
    BACK = J if final else 1
    PER_GROUP = FRONT + BACK
    with nc.Block() as block:
        @block.sync
        def _(sp):
            sp.dma_start(w_own[:, :], W[0:D, :]).then_inc(s_w, 16)
            sp.dma_start(w_acc[:, :], W[D:2 * D, :]).then_inc(s_w, 16)
            sp.dma_start(w_next[:, :], k.L3_gnn_lin1_w[0]).then_inc(s_w, 16)
            sp.dma_start(bias[:, :], b.partition_broadcast(P)).then_inc(s_w, 16)
            feed_items(sp, k, 0, ((k.in_edges, IN_WORDS, ring),), s_ring, s_got, s_here, s_used)

        @block.gpsimd
        def _(pool):
            gather_ahead(pool, k, 0, src[:, :], ring, IN_WORDS, s_ring, 16, got, s_got, s_here, s_used)

        @block.tensor
        def _(pe):
            def transposes(out, of, signal):
                for j in range(J):
                    last = pe.transpose(out[:, j, :], of[:, j, :], k.ident[:, :])
                last.then_inc(signal, 1)

            def next_product(i, u):
                g = i * 2 + u
                pe.wait_ge(s_y, g + 1)
                pe.wait_ge(s_new_t, g + 1)
                transposes(new_p, y[u], s_new_p)
                pe.wait_ge(s_new_t, g + 2)
                pe.wait_ge(s_h, g + 1)
                for j in range(J):
                    last = pe.matmul(h_p[:, j, :], new_t[u][:, j, :], w_next[:, :], start=True, stop=True)
                last.then_inc(s_h_p, 1)

            def group(i, u):
                g = i * 2 + u
                pe.wait_ge(s_own[u], i * 16 + 16)
                pe.wait_ge(s_own_t, g + 1)
                transposes(own_p, own[u], s_own_p)
                pe.wait_ge(s_acc, g + 1)
                pe.wait_ge(s_acc_t, g + 1)
                transposes(acc_p, acc[u], s_acc_p)
                if final and not starts(i, u, 3):
                    next_product(*third_before(i, u))
                pe.wait_ge(s_own_t, g + 2)
                pe.wait_ge(s_acc_t, g + 2)
                pe.wait_ge(s_z, g + 1)
                for j in range(J):
                    pe.matmul(prod[:, j, :], own_t[u][:, j, :], w_own[:, :], start=True, stop=False)
                    last = pe.matmul(prod[:, j, :], acc_t[u][:, j, :], w_acc[:, :], start=False, stop=True)
                last.then_inc(s_prod, 1)

            pe.wait_ge(s_w, 64)
            over_groups(pe, group)
            if final:
                for i, u in ((HALF - 2, 1), (HALF - 1, 0), (HALF - 1, 1)):
                    next_product(i, u)

        @block.scalar
        def _(act):
            act.preload_act_table_set("natural_log_exp_and_others")
            for s in (s_own_t, s_acc_t, s_new_t, s_h):
                act.sem_inc(s, 1)

            def load(i, u):
                act.dma_start(flat(own[u][:, :, :]), own_rows(src, i * 2 + u)).then_inc(s_own[u], 16)

            def scale(i, u):
                g = i * 2 + u
                act.wait_ge(s_mom, g + 1)
                inverse_spread(act, k, moments, log_var, spread, s_log, g).then_inc(s_spread, 1)

            def rectify(i, u):
                free_again(act, s_kept_y[u], i, k.held)
                act.wait_ge(s_z, i * 2 + u + 2)
                act.activation(flat(y[u][:, :, :]), flat(z[:, :, :]), ACT.Relu).then_inc(s_y, 1)

            def keep(i, u):
                g = i * 2 + u
                stand(act, s_y, g + 1, k.held)
                act.dma_start(own_rows(dst, g), flat(y[u][:, :, :])).then_inc(s_kept_y[u], 16)

            def next_rows(i, u):
                g = i * 2 + u
                act.wait_ge(s_new_p, g + 1)
                act.activation(flat(new_t[u][:, :, :]), flat(new_p[:, :, :]), ACT.Copy).then_inc(s_new_t, 1)
                free_again(act, s_kept_h[u], i, k.held)
                act.wait_ge(s_h_p, g + 1)
                act.activation(flat(h[u][:, :, :]), flat(h_p[:, :, :]), ACT.Copy).then_inc(s_h, 1)
                stand(act, s_h, g + 2, k.held)
                act.dma_start(own_rows(k.ha, g), flat(h[u][:, :, :])).then_inc(s_kept_h[u], 16)

            def group(i, u):
                g = i * 2 + u
                stand(act, s_own_p, g + 1, k.held)
                act.activation(flat(own_t[u][:, :, :]), flat(own_p[:, :, :]), ACT.Copy).then_inc(s_own_t, 1)
                if not (isinstance(i, int) and i == HALF - 1):
                    load(i + 1, u)
                if final:
                    act.dma_start(flat(base[u][:, :, :]), own_rows(k.yb, g)).then_inc(s_base[u], 16)
                act.wait_ge(s_acc_p, g + 1)
                act.activation(flat(acc_t[u][:, :, :]), flat(acc_p[:, :, :]), ACT.Copy).then_inc(s_acc_t, 1)
                if final:
                    if not starts(i, u, 3):
                        next_rows(*third_before(i, u))
                    if not starts(i, u, 2):
                        keep(i - 1, u)
                    if not starts(i, u):
                        scale(*before(i, u))
                elif not starts(i, u):
                    rectify(*before(i, u))
                    keep(*before(i, u))

            for u in range(2):
                load(0, u)
            over_groups(act, group)
            if final:
                next_rows(HALF - 2, 1)
                keep(HALF - 1, 0)
                scale(HALF - 1, 1)
                keep(HALF - 1, 1)
                for u in range(2):
                    next_rows(HALF - 1, u)
            else:
                rectify(HALF - 1, 1)
                keep(HALF - 1, 1)
            for u in range(2):
                act.wait_ge(s_kept_y[u], 16 * HALF)
                if final:
                    act.wait_ge(s_kept_h[u], 16 * HALF)

        @block.vector
        def _(dve):
            def with_bias(i, u):
                g = i * 2 + u
                dve.wait_ge(s_prod, g + 1)
                return dve.tensor_tensor(z[:, :, :], prod[:, :, :], bias[:, :].unsqueeze(1).to_broadcast([P, J, D]),
                                         ALU.add)

            def middle(i, u):
                if not starts(i, u):
                    dve.wait_ge(s_y, i * 2 + u)
                with_bias(i, u).then_inc(s_z, 1)

            def add(i, u, c):
                g = i * 2 + u
                c(with_bias(i, u))
                c.wait()
                dve.sem_inc(s_z, 1)
                if not (isinstance(i, int) and i == 0):
                    dve.wait_ge(s_kept_y[u], i * 16)
                    dve.wait_ge(s_new_p, g - 1)
                dve.wait_ge(s_base[u], i * 16 + 16)
                c(dve.scalar_tensor_tensor(out=flat(y[u][:, :, :]), in0=flat(z[:, :, :]), scalar=0.0,
                                           in1=flat(base[u][:, :, :]), op0=ALU.max, op1=ALU.add))
                c.wait()
                spread_stats(dve, k, c, y[u], stats, moments)
                dve.sem_inc(s_mom, 1)

            def finish(i, u, c):
                dve.wait_ge(s_spread, i * 2 + u + 1)
                for j in range(J):
                    c(dve.tensor_scalar(y[u][:, j, :], y[u][:, j, :], moments[:, j, 0:1], spread[:, j:j + 1],
                                        ALU.subtract, ALU.mult))
                c.wait()
                dve.sem_inc(s_y, 1)

            def pass_time(c, n):
                for _ in range(n):
                    c(dve.memset(idle[:, :], 0.0))
                    stand(dve, s_step, c.base + c.n, k.held)

            ends = []

            def group(i, u):
                g = i * 2 + u
                lo, hi = bounds_of(dve, k, i, u, ends)
                stand(dve, s_step, lo * PER_ITEM + g * PER_GROUP + 1, k.held)
                if not starts(i, u, 2):
                    dve.wait_ge(s_acc_p, g - 1)
                c = Chain(dve, s_step, lo * PER_ITEM + g * PER_GROUP + 1)
                c(dve.memset(acc[u][:, :, :], 0.0))
                c(dve.tensor_scalar(inv[:, :], k.in_degree[:, bass.ds(g * J, J)], 1.0, None, ALU.add))
                c.wait()
                c(dve.reciprocal(inv[:, :], inv[:, :]))
                if final:
                    if starts(i, u, 2):
                        pass_time(c, FRONT - 3)
                    else:
                        add(i - 1, u, c)
                c.all(FRONT)
                stand(dve, s_step, lo * PER_ITEM + g * PER_GROUP + 1 + FRONT, k.held)
                with dve.If(lo < hi), dve.Fori(lo, hi) as item:
                    c = Chain(dve, s_step, item * PER_ITEM + g * PER_GROUP + 1 + FRONT)
                    c.wait()
                    dve.wait_ge(s_here, item + 1)
                    rows = got[:, bass.ds(item % DEPTH, 1), :, :].rearrange("p a j d -> p (a j) d")
                    for j in range(J):
                        c(dve.scalar_tensor_tensor(out=acc[u][:, j, :], in0=rows[:, j, :], scalar=inv[:, j:j + 1],
                                                   in1=acc[u][:, j, :], op0=ALU.mult, op1=ALU.add))
                    c.wait()
                    dve.sem_inc(s_used, 1)
                dve.sem_inc(s_acc, 1)
                c = Chain(dve, s_step, hi * PER_ITEM + g * PER_GROUP + 1 + FRONT)
                if final and not starts(i, u, 2):
                    finish(i - 1, u, c)
                else:
                    if not final and not starts(i, u):
                        middle(*before(i, u))
                    pass_time(c, BACK)
                c.all(BACK)

            dve.wait_ge(s_w, 64)
            dve.sem_inc(s_z, 1)
            dve.memset(inv[:, :], 0.0).then_inc(s_step, 1)
            over_groups(dve, group)
            dve.sem_inc(s_used, DEPTH)
            if final:
                c = Chain(dve, s_end)
                for u in range(2):
                    add(HALF - 1, u, c)
                    finish(HALF - 1, u, c)
            else:
                middle(HALF - 1, 1)


def filter_layer(nc, k, l, src, near, dst, near_next):
    final = l == 4
    STEP = CUTOFF / (RADIAL - 1)
    ring = sbuf(nc, "ring", [P, DEPTH, J * IN_WORDS], I32)
    cut = sbuf(nc, "cut", [P, DEPTH, J], F32)
    got = sbuf(nc, "got", [P, DEPTH, J, D], F32)
    rep = sbuf(nc, "rep", [P, J, RADIAL], F32)
    square = sbuf(nc, "square", [P, P], F32)
    radial = sbuf(nc, "radial", [P, P], F32)
    size, decay, soft, hidden = [sbuf(nc, n_, [P, J, P], F32) for n_ in ("size", "decay", "soft", "hidden")]
    filt = sbuf(nc, "filt", [P, J, D], F32)
    msg = sbuf(nc, "msg", [P, J, D], F32)
    factor = sbuf(nc, "factor", [P, J], F32)
    inv = sbuf(nc, "inv", [P, J], F32)
    idle = sbuf(nc, "idle", [1, 1], F32)
    pair = lambda name: [sbuf(nc, f"{name}{u}", [P, J, D], F32) for u in range(2)]
    base, acc, g_soft, g_hidden, y, new_t, h = [
        pair(n_) for n_ in ("base", "acc", "g_soft", "g_hidden", "y", "new_t", "h")]
    oldest = new_t
    g_size, g_decay = [sbuf(nc, n_, [P, J, D], F32) for n_ in ("g_size", "g_decay")]
    stats = sbuf(nc, "stats", [P, J, 6], F32)
    moments = sbuf(nc, "moments", [P, J, 2], F32)
    log_var = sbuf(nc, "log_var", [P, J], F32)
    spread = sbuf(nc, "spread", [P, J], F32)
    fw1 = [sbuf(nc, f"fw1_{j}", [P, D], F32) for j in range(J)]
    fw2, lin2, lin1, gain, shift, fb2 = [
        sbuf(nc, n_, [P, D], F32) for n_ in ("fw2", "lin2", "lin1", "gain", "shift", "fb2")]
    lin2_b = sbuf(nc, "lin2_b", [1, D], F32)
    fb1 = sbuf(nc, "fb1", [P, 1], F32)
    fb1_wide = sbuf(nc, "fb1_wide", [P, P], F32)
    low = sbuf(nc, "low", [P, 1], F32)
    half = sbuf(nc, "half", [P, 1], F32)
    centre = sbuf(nc, "centre", [P, 1], F32)
    rep_p, v_p, w_p, prod, new_p, h_p = [
        psum(nc, n_, [P, J, D], F32) for n_ in ("rep_p", "v_p", "w_p", "prod", "new_p", "h_p")]
    acc_p = [psum(nc, f"acc_p{u}", [P, J, D], F32) for u in range(2)]
    s_got = [sem(nc, f"s_got{j}") for j in range(DEPTH)]
    s_base, s_kept_y, s_kept_h = [[sem(nc, f"{n_}{u}") for u in range(2)] for n_ in ("s_base", "s_kept_y", "s_kept_h")]
    (s_w, s_set, s_start, s_ring, s_here, s_used, s_rep, s_rep_p, s_square, s_radial, s_v, s_size, s_decay, s_soft,
     s_hidden, s_w_p, s_filt, s_item, s_group, s_acc, s_acc_p, s_g_size, s_g_decay, s_g_soft, s_g_hidden, s_prod, s_sum, s_mom,
     s_log, s_spread, s_y, s_new_p, s_new_t, s_h_p, s_h, s_end) = [sem(nc, n_) for n_ in (
         "s_w", "s_set", "s_start", "s_ring", "s_here", "s_used", "s_rep", "s_rep_p", "s_square", "s_radial", "s_v",
         "s_size", "s_decay", "s_soft", "s_hidden", "s_w_p", "s_filt", "s_item", "s_group", "s_acc", "s_acc_p", "s_g_size",
         "s_g_decay", "s_g_soft", "s_g_hidden", "s_prod", "s_sum", "s_mom", "s_log", "s_spread", "s_y", "s_new_p",
         "s_new_t", "s_h_p", "s_h", "s_end")]
    LOADS = (J + 8) * 16
    NORMS = 2 if final else 1
    PER_ITEM = 2 + J
    FRONT = 3 + 1 + 2 * J
    BACK = J + 2 + (1 + 3 * J if final else 0)
    PER_GROUP = FRONT + BACK
    with nc.Block() as block:
        @block.sync
        def _(sp):
            sp.wait_ge(s_set, J)
            for j in range(J):
                sp.dma_start(fw1[j][j * RADIAL:(j + 1) * RADIAL, :], k.L3_gnn_fw1[l]).then_inc(s_w, 16)
            for to, of in ((fw2, k.L3_gnn_fw2[l]), (lin2, k.L3_gnn_lin2_w[l]), (lin1, k.L3_gnn_lin1_w[(l + 1) % 5])):
                sp.dma_start(to[:, :], of).then_inc(s_w, 16)
            for to, of in ((gain, k.L3_gnn_ln_g[l]), (shift, k.L3_gnn_ln_b[l]), (fb2, k.L3_gnn_fb2[l])):
                sp.dma_start(to[:, :], of.partition_broadcast(P)).then_inc(s_w, 16)
            sp.dma_start(fb1[:, :], k.L3_gnn_fb1[l].rearrange("(d a) -> d a", a=1)).then_inc(s_w, 16)
            sp.dma_start(lin2_b[:, :], k.L3_gnn_lin2_b[l].rearrange("(a d) -> a d", a=1)).then_inc(s_w, 16)
            feed_items(sp, k, 0, ((k.in_edges, IN_WORDS, ring), (k.cutoffs, 1, cut)),
                       s_ring, s_got, s_here, s_used)

        @block.gpsimd
        def _(pool):
            gather_ahead(pool, k, 0, near[:, :], ring, IN_WORDS, s_ring, 32, got, s_got, s_here, s_used)

        @block.tensor
        def _(pe):
            def transposes(out, of, signal):
                for j in range(J):
                    last = pe.transpose(out[:, j, :], of[:, j, :], k.ident[:, :])
                last.then_inc(signal, 1)

            def turn(i):
                pe.wait_ge(s_rep, i + 1)
                pe.wait_ge(s_square, i + 1)
                pe.transpose(rep_p[:, 0, :], rep[:, :, :].rearrange("p j r -> p (j r)"), k.ident[:, :]
                             ).then_inc(s_rep_p, 1)

            def first_product(i):
                pe.wait_ge(s_radial, i + 1)
                pe.wait_ge(s_hidden, i + 1)
                for j in range(J):
                    last = pe.matmul(v_p[:, j, :], fw1[j][:, :], radial[:, :], start=True, stop=True)
                last.then_inc(s_v, 1)

            def second_product(i):
                pe.wait_ge(s_hidden, i + 2)
                pe.wait_ge(s_filt, i + 1)
                for j in range(J):
                    last = pe.matmul(w_p[:, j, :], hidden[:, j, :], fw2[:, :], start=True, stop=True)
                last.then_inc(s_w_p, 1)

            def mix(i, u):
                g = i * 2 + u
                pe.wait_ge(s_g_hidden, g + 1)
                pe.wait_ge(s_sum, g + 1)
                for j in range(J):
                    pe.matmul(prod[:, j, :], g_hidden[u][:, j, :], lin2[:, :], start=True, stop=False)
                    last = pe.matmul(prod[:, j, :], k.ones[0:1, 0:P], lin2_b[0:1, :], start=False, stop=True)
                last.then_inc(s_prod, 1)

            def turn_new(i, u):
                g = i * 2 + u
                pe.wait_ge(s_y, g + 1)
                pe.wait_ge(s_new_t, g + 1)
                transposes(new_p, y[u], s_new_p)

            def next_product(i, u):
                g = i * 2 + u
                pe.wait_ge(s_new_t, g + 2)
                pe.wait_ge(s_h, g + 1)
                for j in range(J):
                    last = pe.matmul(h_p[:, j, :], new_t[u][:, j, :], lin1[:, :], start=True, stop=True)
                last.then_inc(s_h_p, 1)

            ends = []

            def group(i, u):
                g = i * 2 + u
                if not final and not starts(i, u, 3):
                    turn_new(*third_before(i, u))
                    next_product(*third_before(i, u))
                    pe.sem_inc(k.held, 1)
                lo, hi = bounds_of(pe, k, i, u, ends)
                with pe.If(lo < hi), pe.Fori(lo, hi) as item:
                    turn(item + 2)
                    first_product(item + 2)
                    second_product(item + 1)
                pe.wait_ge(s_acc, g + 1)
                if not starts(i, u, 2):
                    pe.wait_ge(s_g_hidden, g - 1)
                transposes(acc_p[u], acc[u], s_acc_p)
                if not starts(i, u):
                    mix(*before(i, u))
                pe.sem_inc(k.held, 1)

            pe.wait_ge(s_start, 1)
            pe.matmul(w_p[:, 0, :], fb1_wide[:, :], fw2[:, :], start=True, stop=True).then_inc(s_end, 1)
            pe.wait_ge(s_start, 2)
            turn(0)
            first_product(0)
            turn(1)
            first_product(1)
            second_product(0)
            pe.sem_inc(k.held, 1)
            over_groups(pe, group)
            mix(HALF - 1, 1)
            if not final:
                for i, u in ((HALF - 2, 1), (HALF - 1, 0), (HALF - 1, 1)):
                    turn_new(i, u)
                    next_product(i, u)

        @block.scalar
        def _(act):
            act.preload_act_table_set("natural_log_exp_and_others")
            for s in (s_square, s_new_t, s_h):
                act.sem_inc(s, 1)

            def load(i, u):
                act.dma_start(flat(base[u][:, :, :]), own_rows(src, i * 2 + u)).then_inc(s_base[u], 16)
                if final:
                    act.dma_start(flat(oldest[u][:, :, :]), own_rows(k.ya, i * 2 + u)).then_inc(s_base[u], 16)

            def rbf(i):
                act.wait_ge(s_rep_p, i + 1)
                act.activation(square[:, :], rep_p[:, 0, :], ACT.Square, bias=centre[:, 0:1]).then_inc(s_square, 1)
                act.wait_ge(s_square, i + 2)
                act.activation(radial[:, :], square[:, :], ACT.Exp, scale=-0.5 / STEP ** 2).then_inc(s_radial, 1)

            def softplus(i, early=False):
                act.wait_ge(s_v, i + 1)
                act.activation(flat(size[:, :, :]), flat(v_p[:, :, :]), ACT.Abs, bias=fb1[:, 0:1]).then_inc(s_size, 1)
                act.wait_ge(s_size, i + 1)
                if not early:
                    act.wait_ge(s_soft, i)
                act.activation(flat(decay[:, :, :]), flat(size[:, :, :]), ACT.Exp, scale=-1.0).then_inc(s_decay, 1)
                act.wait_ge(s_decay, i + 1)
                act.wait_ge(s_hidden, i + 1)
                act.activation(flat(soft[:, :, :]), flat(decay[:, :, :]), ACT.Ln, bias=half[:, 0:1], scale=0.5
                               ).then_inc(s_soft, 1)

            def group_softplus(i, u):
                g = i * 2 + u
                act.wait_ge(s_acc_p, g + 1)
                act.activation(flat(g_size[:, :, :]), flat(acc_p[u][:, :, :]), ACT.Abs).then_inc(s_g_size, 1)
                act.wait_ge(s_g_size, g + 1)
                if not starts(i, u):
                    act.wait_ge(s_g_soft, g)
                act.activation(flat(g_decay[:, :, :]), flat(g_size[:, :, :]), ACT.Exp, scale=-1.0
                               ).then_inc(s_g_decay, 1)
                act.wait_ge(s_g_decay, g + 1)
                act.activation(flat(g_soft[u][:, :, :]), flat(g_decay[:, :, :]), ACT.Ln, bias=half[:, 0:1], scale=0.5
                               ).then_inc(s_g_soft, 1)

            def scale(i, u, n):
                g = i * 2 + u
                act.wait_ge(s_mom, g * NORMS + n + 1)
                inverse_spread(act, k, moments, log_var, spread, s_log, g * NORMS + n).then_inc(s_spread, 1)

            def keep(i, u):
                g = i * 2 + u
                stand(act, s_y, g + 1, k.held)
                act.dma_start(own_rows(dst, g), flat(y[u][:, :, :])).then_inc(s_kept_y[u], 16)

            def next_rows(i, u):
                g = i * 2 + u
                act.wait_ge(s_new_p, g + 1)
                act.activation(flat(new_t[u][:, :, :]), flat(new_p[:, :, :]), ACT.Copy).then_inc(s_new_t, 1)
                free_again(act, s_kept_h[u], i, k.held)
                act.wait_ge(s_h_p, g + 1)
                act.activation(flat(h[u][:, :, :]), flat(h_p[:, :, :]), ACT.Copy).then_inc(s_h, 1)
                stand(act, s_h, g + 2, k.held)
                act.dma_start(own_rows(near_next, g), flat(h[u][:, :, :])).then_inc(s_kept_h[u], 16)

            ends = []

            def group(i, u):
                if not final and not starts(i, u, 3):
                    keep(*third_before(i, u))
                    next_rows(*third_before(i, u))
                lo, hi = bounds_of(act, k, i, u, ends)
                if not starts(i, u, 2):
                    scale(i - 1, u, 0)
                    act.sem_inc(k.held, 1)
                with act.If(lo < hi), act.Fori(lo, hi) as item:
                    rbf(item + 2)
                    softplus(item + 2)
                group_softplus(i, u)
                if final and not starts(i, u, 2):
                    scale(i - 1, u, 1)
                    keep(i - 1, u)
                if not starts(i, u, 2):
                    load(i, u)
                act.sem_inc(k.held, 1)

            act.wait_ge(s_start, 2)
            for u in range(2):
                load(0, u)
            rbf(0)
            softplus(0, True)
            rbf(1)
            softplus(1)
            over_groups(act, group)
            if not final:
                keep(HALF - 2, 1)
                next_rows(HALF - 2, 1)
            for u in range(2):
                for n in range(NORMS):
                    scale(HALF - 1, u, n)
                keep(HALF - 1, u)
                if not final:
                    next_rows(HALF - 1, u)
            for u in range(2):
                act.wait_ge(s_kept_y[u], 16 * HALF)
                if not final:
                    act.wait_ge(s_kept_h[u], 16 * HALF)

        @block.vector
        def _(dve):
            def weights(i, slot):
                dve.wait_ge(s_ring, i * 32 + 32)
                half_ring = ring[:, slot, :].rearrange("p a (j w) -> p (a j) w", w=IN_WORDS)
                dve.tensor_copy(rep[:, :, :], half_ring[:, :, 1:2].bitcast(F32).to_broadcast([P, J, RADIAL])
                                ).then_inc(s_rep, 1)

            def hide(i):
                dve.wait_ge(s_soft, i + 1)
                dve.scalar_tensor_tensor(out=flat(hidden[:, :, :]), in0=flat(v_p[:, :, :]), scalar=low[:, 0:1],
                                         in1=flat(soft[:, :, :]), op0=ALU.max, op1=ALU.add).then_inc(s_hidden, 1)

            def item_(i, g, u):
                c = Chain(dve, s_item, i * PER_ITEM + 1)
                c.wait()
                dve.wait_ge(s_rep_p, i + 2)
                weights(i + 2, bass.ds((i + 2) % DEPTH, 1))
                dve.wait_ge(s_w_p, i + 1)
                hide(i + 1)
                c(dve.tensor_tensor(factor[:, :], cut[:, bass.ds(i % DEPTH, 1), :].rearrange("p a j -> p (a j)"),
                                    inv[:, :], ALU.mult))
                dve.wait_ge(s_w_p, i + 1)
                dve.tensor_tensor(filt[:, :, :], w_p[:, :, :], fb2[:, :].unsqueeze(1).to_broadcast([P, J, D]), ALU.add
                                  ).then_inc(s_filt, 1)
                dve.wait_ge(s_filt, i + 2)
                dve.wait_ge(s_here, i + 1)
                c(dve.tensor_tensor(msg[:, :, :], filt[:, :, :],
                                    got[:, bass.ds(i % DEPTH, 1), :, :].rearrange("p a j d -> p (a j) d"), ALU.mult))
                c.wait()
                dve.sem_inc(s_used, 1)
                for j in range(J):
                    c(dve.scalar_tensor_tensor(out=acc[u][:, j, :], in0=msg[:, j, :], scalar=factor[:, j:j + 1],
                                               in1=acc[u][:, j, :], op0=ALU.mult, op1=ALU.add))
                c.all(PER_ITEM)

            def mid(i, u):
                g = i * 2 + u
                dve.wait_ge(s_g_soft, g + 1)
                dve.scalar_tensor_tensor(out=flat(g_hidden[u][:, :, :]), in0=flat(acc_p[u][:, :, :]), scalar=0.0,
                                         in1=flat(g_soft[u][:, :, :]), op0=ALU.max, op1=ALU.add
                                         ).then_inc(s_g_hidden, 1)

            def add(i, u, c):
                g = i * 2 + u
                dve.wait_ge(s_prod, g + 1)
                if not (isinstance(i, int) and i == 0):
                    dve.wait_ge(s_kept_y[u], i * 16)
                    if not final:
                        dve.wait_ge(s_new_p, g - 1)
                dve.wait_ge(s_base[u], (i * 16 + 16) * NORMS)
                c(dve.tensor_tensor(flat(y[u][:, :, :]), flat(prod[:, :, :]), flat(base[u][:, :, :]), ALU.add))
                c.wait()
                dve.sem_inc(s_sum, 1)
                spread_stats(dve, k, c, y[u], stats, moments)
                dve.sem_inc(s_mom, 1)

            def normalise(i, u, c, n):
                dve.wait_ge(s_spread, (i * 2 + u) * NORMS + n + 1)
                for j in range(J):
                    c(dve.tensor_scalar(y[u][:, j, :], y[u][:, j, :], moments[:, j, 0:1], spread[:, j:j + 1],
                                        ALU.subtract, ALU.mult))
                c.wait()

            def finish(i, u, c):
                normalise(i, u, c, 0)
                for with_, op in ((gain, ALU.mult), (shift, ALU.add)):
                    c(dve.tensor_tensor(y[u][:, :, :], y[u][:, :, :],
                                        with_[:, :].unsqueeze(1).to_broadcast([P, J, D]), op))
                    c.wait()
                if final:
                    c(dve.tensor_tensor(flat(y[u][:, :, :]), flat(y[u][:, :, :]), flat(oldest[u][:, :, :]), ALU.add))
                    c.wait()
                    spread_stats(dve, k, c, y[u], stats, moments)
                    dve.sem_inc(s_mom, 1)
                    normalise(i, u, c, 1)
                dve.sem_inc(s_y, 1)

            def pass_time(c, n):
                for _ in range(n):
                    c(dve.memset(idle[:, :], 0.0))
                    stand(dve, s_group, c.base + c.n, k.held)

            ends = []

            def group(i, u):
                g = i * 2 + u
                dve.wait_ge(s_group, g * PER_GROUP + 1)
                if not starts(i, u, 2):
                    dve.wait_ge(s_acc_p, g - 1)
                c = Chain(dve, s_group, g * PER_GROUP + 1)
                c(dve.memset(acc[u][:, :, :], 0.0))
                c(dve.tensor_scalar(inv[:, :], k.in_degree[:, bass.ds(g * J, J)], 1.0, None, ALU.max))
                c.wait()
                c(dve.reciprocal(inv[:, :], inv[:, :]))
                lo, hi = bounds_of(dve, k, i, u, ends)
                if not starts(i, u, 2):
                    add(i - 1, u, c)
                else:
                    pass_time(c, FRONT - 3)
                c.all(FRONT)
                stand(dve, s_group, g * PER_GROUP + 1 + FRONT, k.held)
                with dve.If(lo < hi), dve.Fori(lo, hi) as item:
                    item_(item, g, u)
                dve.wait_ge(s_item, hi * PER_ITEM + 1)
                c = Chain(dve, s_group, g * PER_GROUP + 1 + FRONT)
                dve.sem_inc(s_acc, 1)
                if not starts(i, u):
                    mid(*before(i, u))
                if not starts(i, u, 2):
                    finish(i - 1, u, c)
                else:
                    pass_time(c, BACK)
                c.all(BACK)

            for j in range(J):
                dve.memset(fw1[j][:, :], 0.0).then_inc(s_set, 1)
            dve.wait_ge(s_w, LOADS)
            c = Chain(dve, s_end)
            c.base = 1
            c(dve.memset(half[:, :], 0.5))
            c(dve.tensor_scalar(low[:, :], fb1[:, :], -1.0, None, ALU.mult))
            c(dve.tensor_scalar(fb1_wide[:, :], k.ones[:, 0:P], fb1[:, 0:1], None, ALU.mult))
            c(dve.tensor_scalar(centre[:, :], k.radial_of[:, :], -STEP, None, ALU.mult))
            dve.wait_ge(s_end, 4)
            dve.sem_inc(s_start, 1)
            c.wait()
            c(dve.tensor_tensor(fb2[:, :], w_p[:, 0, :], fb2[:, :], ALU.add))
            c(dve.memset(inv[:, :], 0.0))
            c.wait()
            for s in (s_start, s_hidden, s_filt, s_sum):
                dve.sem_inc(s, 1)
            dve.memset(factor[:, :], 0.0).then_inc(s_item, 1)
            dve.memset(idle[:, :], 0.0).then_inc(s_group, 1)
            weights(0, slice(0, 1))
            dve.wait_ge(s_rep_p, 1)
            weights(1, slice(1, 2))
            hide(0)
            dve.sem_inc(k.held, 1)
            over_groups(dve, group)
            dve.sem_inc(s_used, DEPTH)
            mid(HALF - 1, 1)
            c = Chain(dve, s_end, c.base + c.n)
            c.wait()
            for u in range(2):
                add(HALF - 1, u, c)
                finish(HALF - 1, u, c)


def deliver(nc, k):
    U = 2
    to = [sbuf(nc, f"to{u}", [P, J], U32) for u in range(U)]
    rows = [sbuf(nc, f"rows{u}", [P, J, D], F32) for u in range(U)]
    s_to = sem(nc, "s_to")
    s_rows, s_kept = [[sem(nc, f"{n_}{u}") for u in range(U)] for n_ in ("s_rows", "s_kept")]
    TAIL_TILES = (N - (NG - 1) * G) // P
    TAIL_ROWS = N - (NG - 1) * G - TAIL_TILES * P
    with nc.Block() as block:
        @block.vector
        def _(dve):
            for u in range(U):
                dve.tensor_copy(to[u][:, :], k.row_d[:, u * J:(u + 1) * J]).then_inc(s_to, 1)
            with dve.Fori(1, NG // U) as i:
                for u in range(U):
                    dve.wait_ge(s_rows[u], i * 16 * J)
                    dve.tensor_copy(to[u][:, :], k.row_d[:, bass.ds((i * U + u) * J, J)]).then_inc(s_to, 1)

        @block.gpsimd
        def _(pool):
            def gather(i, u):
                stand(pool, s_to, i * U + u + 1, k.held)
                for j in range(J):
                    pool.indirect_dma_start(rows[u][:, j, :], None, k.yb[:, :],
                                            bass.IndirectOffsetOnAxis(ap=to[u][:, j:j + 1], axis=0)
                                            ).then_inc(s_rows[u], 16)

            for u in range(U):
                gather(0, u)
            with pool.Fori(1, NG // U) as i:
                for u in range(U):
                    stand(pool, s_kept[u], i * 16, k.held)
                    gather(i, u)

        @block.sync
        def _(sp):
            def store(i, u):
                stand(sp, s_rows[u], i * 16 * J + 16 * J, k.held)
                sp.dma_start(k.out[bass.ds((i * U + u) * G, G), :].rearrange("(j p) d -> p j d", p=P),
                             rows[u][:, :, :]).then_inc(s_kept[u], 16)

            with sp.Fori(0, NG // U - 1) as i:
                for u in range(U):
                    store(i, u)
            store(NG // U - 1, 0)
            last = (NG - 1) * G
            stand(sp, s_rows[1], NG // U * 16 * J, k.held)
            sp.dma_start(k.out[last:last + TAIL_TILES * P, :].rearrange("(j p) d -> p j d", p=P),
                         rows[1][:, 0:TAIL_TILES, :]).then_inc(s_kept[1], 16)
            sp.dma_start(k.out[last + TAIL_TILES * P:N, :], rows[1][0:TAIL_ROWS, TAIL_TILES, :]
                         ).then_inc(s_kept[1], 16)
            sp.wait_ge(s_kept[0], 16 * NG // U)
            sp.wait_ge(s_kept[1], 16 * NG // U + 16)


XW = D + 2


def persistent(nc, k):
    k.high, k.low, k.rank, k.degree, k.column = [
        [sbuf(nc, f"{name}{q}", [P, NT], F32) for q in range(2)]
        for name in ("high", "low", "rank", "degree", "column")]
    k.held = sem(nc, "held")
    k.lane = [sbuf(nc, f"lane{q}", [P, NT], I32) for q in range(2)]
    k.start = [sbuf(nc, f"start{q}", [1, P], I32) for q in range(2)]
    k.key = [sbuf(nc, f"key{q}", [P, NT + J], U32) for q in range(2)]
    k.past = sbuf(nc, "past", [P, NT], I32)
    k.row_d = sbuf(nc, "row_d", [P, NT], F32)
    k.row_s = sbuf(nc, "row_s", [P, NT], F32)
    k.in_degree = sbuf(nc, "in_degree", [P, NT], F32)
    k.score = sbuf(nc, "score", [P, 2, NT], F32)
    k.weight = sbuf(nc, "weight", [P, NT], F32)
    k.XW = XW
    dram = lambda name, shape, dt: nc.dram_tensor(name, shape, dt).ap()
    k.low_rows = [dram(f"low_rows{q}", [4 * P, P], F32) for q in range(2)]
    k.x_pad = dram("x_pad", [NR, D], F32)
    k.h0 = dram("h0", [NR + 1, D], F32)
    k.mix = dram("mix", [NR + 1, D], F32)
    k.mean_w = [k.L2_gnn_W0, k.L2_gnn_W1, k.L2_gnn_W2]
    k.mean_b = [k.L2_gnn_b0, k.L2_gnn_b1, k.L2_gnn_b2]
    k.ha = dram("ha", [NR + 1, D], F32)
    k.ya = dram("ya", [NR + 1, D], F32)
    k.yb = dram("yb", [NR + 1, D], F32)
    k.yc = dram("yc", [NR + 1, D], F32)
    k.hb = dram("hb", [NR + 1, D], F32)
    k.xd = dram("xd", [NR + 1, XW], F32)
    k.by_src = dram("by_src", [NR, 4], I32)
    k.by_dst = dram("by_dst", [NR, 4], I32)
    k.in_edges = dram("in_edges", [P * COLS, IN_WORDS], I32)
    k.cutoffs = dram("cutoffs", [P * COLS, 1], F32)
    k.out_edges = dram("out_edges", [P * COLS, OUT_WORDS], I32)

STAGES = [("load_keys", load_keys), ("rank_edges", rank_edges), ("sort_nodes", sort_nodes), ("project", project),
          ("lay_out_edges", lay_out_edges), ("cut_off", cut_off), ("attend", attend),
          ("join_attention", join_attention), ("hyperbolic", hyperbolic),
          ("mean0", lambda nc, k: mean_layer(nc, k, 0, k.yb, k.ya)),
          ("mean1", lambda nc, k: mean_layer(nc, k, 1, k.ya, k.yc)),
          ("mean2", lambda nc, k: mean_layer(nc, k, 2, k.yc, k.ya)),
          ("filter0", lambda nc, k: filter_layer(nc, k, 0, k.ya, k.ha, k.yb, k.hb)),
          ("filter1", lambda nc, k: filter_layer(nc, k, 1, k.yb, k.hb, k.yc, k.ha)),
          ("filter2", lambda nc, k: filter_layer(nc, k, 2, k.yc, k.ha, k.yb, k.hb)),
          ("filter3", lambda nc, k: filter_layer(nc, k, 3, k.yb, k.hb, k.yc, k.ha)),
          ("filter4", lambda nc, k: filter_layer(nc, k, 4, k.yc, k.ha, k.yb, None)),
          ("deliver", deliver)]


INPUTS = ("x", "src", "dst", "edge_weight", "L0_gnn_W", "L0_gnn_b", "L0_gnn_a1_w", "L0_gnn_a1_b", "L0_gnn_a2_w",
          "L0_gnn_a2_b", "L2_gnn_W0", "L2_gnn_b0", "L2_gnn_W1", "L2_gnn_b1", "L2_gnn_W2", "L2_gnn_b2",
          "L3_gnn_fw1", "L3_gnn_fb1", "L3_gnn_fw2", "L3_gnn_fb2", "L3_gnn_lin1_w", "L3_gnn_lin2_w",
          "L3_gnn_lin2_b", "L3_gnn_ln_g", "L3_gnn_ln_b")


class Shared:
    pass


def program(nc, arrays, out):
    k = Shared()
    k.out = out
    (k.x, k.src, k.dst, k.edge_weight, k.L0_gnn_W, k.L0_gnn_b, k.L0_gnn_a1_w, k.L0_gnn_a1_b, k.L0_gnn_a2_w,
     k.L0_gnn_a2_b, k.L2_gnn_W0, k.L2_gnn_b0, k.L2_gnn_W1, k.L2_gnn_b1, k.L2_gnn_W2, k.L2_gnn_b2,
     k.L3_gnn_fw1, k.L3_gnn_fb1, k.L3_gnn_fw2, k.L3_gnn_fb2, k.L3_gnn_lin1_w, k.L3_gnn_lin2_w,
     k.L3_gnn_lin2_b, k.L3_gnn_ln_g, k.L3_gnn_ln_b) = arrays
    with nc.cleanup_on_exit():
        persistent(nc, k)
        constants(nc, k)
        for _, stage in STAGES:
            with nc.cleanup_on_exit():
                stage(nc, k)


def kernel(**inputs):
    import concourse.bacc as bacc
    from concourse.bass_utils import run_bass_kernel_spmd

    nc = bacc.Bacc("TRN2", target_bir_lowering=False, num_devices=1)
    arrays, tensors = {}, []
    for name in INPUTS:
        a = np.ascontiguousarray(inputs[name])
        arrays[f"in_{name}_dram"] = a
        tensors.append(nc.dram_tensor(f"in_{name}_dram", a.shape, mybir.dt.from_np(a.dtype),
                                      kind="ExternalInput").ap())
    out = nc.dram_tensor("out_0_dram", (N, D), F32, kind="ExternalOutput").ap()
    program(nc, tensors, out)
    results = run_bass_kernel_spmd(nc, [arrays], core_ids=[0])
    return results.results[0]["out_0_dram"]
```
